# Optimizing a Trainium2 kernel written in Bass

```python
import numpy as np
import jax
import jax.numpy as jnp

def _softmax(x, axis=-1):
    return jax.nn.softmax(x, axis=axis)

def _gelu(x):
    return jax.nn.gelu(x, approximate=True)

def _silu(x):
    return jax.nn.silu(x)

def _sigmoid(x):
    return jax.nn.sigmoid(x)

def _layernorm(x, axis=-1, eps=1e-05):
    m = jnp.mean(x, axis=axis, keepdims=True)
    v = jnp.var(x, axis=axis, keepdims=True)
    return (x - m) / jnp.sqrt(v + eps)

def _scatter_add(tgt, idx, src, axis=0):
    return tgt.at[idx].add(src)

def _segment_sum(src, seg, n):
    return jax.ops.segment_sum(src, seg, n)
kernel_name = 'mk_decoder_preln_d1_seqx_r4_7399e6'

def setup_inputs(seed: int=0):
    np.random.seed(seed)
    _w = jnp.asarray

    def _rec_inputs():
        import jax
        import jax.numpy as jnp
        _rk = jax.random.key(seed)
        x = -0.0003929 + 0.9999 * jax.random.normal(jax.random.fold_in(_rk, 1), (4, 512, 1024), jnp.float32)
        _lenS = 512 - jax.random.randint(jax.random.fold_in(_rk, 7), (4,), 0, max(1, 512 // 4) + 1, jnp.int32)
        _lenS2 = 1601 - jax.random.randint(jax.random.fold_in(_rk, 8), (4,), 0, max(1, 1601 // 4) + 1, jnp.int32)
        _ctx_1024P = jax.random.normal(jax.random.fold_in(_rk, 11), (4, 16, 256), jnp.float32)
        _ctx_1024c = jax.random.dirichlet(jax.random.fold_in(_rk, 511), 0.3 * jnp.ones((16,), jnp.float32), (4, 1601))
        _ctx_1024t = jnp.einsum('bsk,bkd->bsd', _ctx_1024c, _ctx_1024P)
        _ctx_1024t = _ctx_1024t * jax.lax.rsqrt(jnp.mean(jnp.square(_ctx_1024t)) + 1e-12) * 0.953939
        ctx_1024 = -1.39393e-06 + 0.999914 * (_ctx_1024t + 0.3 * jax.random.normal(jax.random.fold_in(_rk, 611), (4, 1601, 256), jnp.float32))
        _validS = jnp.arange(512)[None, :] < _lenS[:, None]
        _validS2 = jnp.arange(1601)[None, :] < _lenS2[:, None]
        _causal = jnp.tril(jnp.ones((512, 512), dtype=bool))
        mask_SxS2_ff0 = jnp.where(jnp.ones((512, 1601), dtype=bool), 0.0, -1000000000.0).astype(jnp.float32)
        return (x, ctx_1024, mask_SxS2_ff0)
    x, ctx_1024, mask_SxS2_ff0 = _rec_inputs()

    def _L0_attn_setup():
        import math
        import jax, jax.numpy as jnp
        import numpy as np

        def _rope_tables(T, h, dtype):
            pos = jnp.arange(T, dtype=jnp.float32)
            thetas = 1.0 / 10000.0 ** (jnp.arange(0, h, 2, dtype=jnp.float32) / h)
            pt = jnp.outer(pos, thetas)
            pt = jnp.concatenate([pt, pt], axis=-1)
            return (jnp.sin(pt).astype(dtype), jnp.cos(pt).astype(dtype))

        def _apply_rope(x, sin, cos):
            h = x.shape[-1]
            rot = jnp.concatenate([-x[..., h // 2:], x[..., :h // 2]], axis=-1)
            return x * cos + rot * sin
        key = jax.random.key(seed)
        ks = jax.random.split(key, 5)
        B, T, C = (2, 512, 1024)
        s = 1.0 / math.sqrt(C)
        return {'x': jax.random.normal(ks[0], (B, T, C), dtype=jnp.float32), 'wq': jax.random.normal(ks[1], (C, C), dtype=jnp.float32) * s, 'wk': jax.random.normal(ks[2], (C, C), dtype=jnp.float32) * s, 'wv': jax.random.normal(ks[3], (C, C), dtype=jnp.float32) * s, 'wo': jax.random.normal(ks[4], (C, C), dtype=jnp.float32) * s}
    _L0_attn_all = _L0_attn_setup()
    _L0_attn_in = {k: v for k, v in _L0_attn_all.items() if k in ('wq', 'wk', 'wv', 'wo')}
    del _L0_attn_all

    def _L0_xattn_setup():
        import math
        import jax, jax.numpy as jnp
        import numpy as np
        N_HEADS = 32
        N_KV_HEADS = 8
        N_REP = N_HEADS // N_KV_HEADS
        HEAD_DIM = 1024 // N_HEADS
        key = jax.random.key(seed)
        kq, kk, kv = jax.random.split(key, 3)
        B, S, T = (2, 512, 512)
        q = jax.random.normal(kq, (B, S, N_HEADS * HEAD_DIM), dtype=jnp.float32)
        k = jax.random.normal(kk, (B, T, N_KV_HEADS * HEAD_DIM), dtype=jnp.float32)
        v = jax.random.normal(kv, (B, T, N_KV_HEADS * HEAD_DIM), dtype=jnp.float32)
        mask = jnp.zeros((S, T), dtype=jnp.float32)
        return {'q': q, 'k': k, 'v': v, 'start_pos': 0, 'mask': mask}
    _L0_xattn_all = _L0_xattn_setup()
    _L0_xattn_in = {k: v for k, v in _L0_xattn_all.items() if k in ()}
    del _L0_xattn_all

    def _L0_ffn_setup():
        import jax, jax.numpy as jnp
        import numpy as np
        HID, BOT, RDIM, NSLOT, K, VB = (1024, 64, 48, 256, 8, 64)
        TAU_LOW, TAU_HIGH, EARLY_EXIT = (0.5, 2.0, 0.05)

        def _uncertainty(h, Wu1, bu1, Wu2, bu2):
            var = jnp.var(h, axis=-1)
            log_var = jnp.log1p(var)
            norm_var = log_var / (jnp.mean(log_var) + 1e-06)
            learned = (jax.nn.gelu(h @ Wu1.T + bu1) @ Wu2.T + bu2)[..., 0]
            return jnp.clip(norm_var * 0.5 + jax.nn.sigmoid(learned) * 2.5, 0.0, 5.0)
        key = jax.random.key(seed)
        ks = jax.random.split(key, 12)
        B, S = (2, 512)
        return {'hidden_states': jax.random.normal(ks[0], (B, S, HID), dtype=jnp.float32), 'Wq': jax.random.normal(ks[1], (BOT, HID), dtype=jnp.float32) / np.sqrt(HID), 'Wr': jax.random.normal(ks[2], (RDIM, BOT), dtype=jnp.float32) / np.sqrt(BOT), 'aux_keys': jax.random.normal(ks[3], (NSLOT, BOT), dtype=jnp.float32) * 0.01, 'aux_values': jax.random.normal(ks[4], (NSLOT, HID), dtype=jnp.float32) * 0.02, 'Wvd': jax.random.normal(ks[5], (VB, HID), dtype=jnp.float32) * 0.1 / np.sqrt(HID), 'Wvu': jax.random.normal(ks[6], (HID, VB), dtype=jnp.float32) * 0.1 / np.sqrt(VB), 'Wu1': jax.random.normal(ks[7], (HID // 4, HID), dtype=jnp.float32) / np.sqrt(HID), 'bu1': jnp.zeros((HID // 4,), dtype=jnp.float32), 'Wu2': jax.random.normal(ks[8], (1, HID // 4), dtype=jnp.float32) * 0.01, 'bu2': jnp.zeros((1,), dtype=jnp.float32), 'gate_w1': jnp.float32(0.5), 'gate_bias': jnp.float32(-1.0), 'log_rel': jnp.zeros((NSLOT,), dtype=jnp.float32)}
    _L0_ffn_all = _L0_ffn_setup()
    _L0_ffn_in = {k: v for k, v in _L0_ffn_all.items() if k in ('Wq', 'Wr', 'aux_keys', 'aux_values', 'Wvd', 'Wvu', 'Wu1', 'bu1', 'Wu2', 'bu2', 'gate_w1', 'gate_bias', 'log_rel')}
    del _L0_ffn_all
    return {'x': x, 'ctx_1024': ctx_1024, 'mask_SxS2_ff0': mask_SxS2_ff0, 'L0_attn_wq': _L0_attn_in['wq'], 'L0_attn_wk': _L0_attn_in['wk'], 'L0_attn_wv': _L0_attn_in['wv'], 'L0_attn_wo': _L0_attn_in['wo'], 'L0_ffn_Wq': _L0_ffn_in['Wq'], 'L0_ffn_Wr': _L0_ffn_in['Wr'], 'L0_ffn_aux_keys': _L0_ffn_in['aux_keys'], 'L0_ffn_aux_values': _L0_ffn_in['aux_values'], 'L0_ffn_Wvd': _L0_ffn_in['Wvd'], 'L0_ffn_Wvu': _L0_ffn_in['Wvu'], 'L0_ffn_Wu1': _L0_ffn_in['Wu1'], 'L0_ffn_bu1': _L0_ffn_in['bu1'], 'L0_ffn_Wu2': _L0_ffn_in['Wu2'], 'L0_ffn_bu2': _L0_ffn_in['bu2'], 'L0_ffn_gate_w1': _L0_ffn_in['gate_w1'], 'L0_ffn_gate_bias': _L0_ffn_in['gate_bias'], 'L0_ffn_log_rel': _L0_ffn_in['log_rel']}

def reference(x, ctx_1024, mask_SxS2_ff0, L0_attn_wq, L0_attn_wk, L0_attn_wv, L0_attn_wo, L0_ffn_Wq, L0_ffn_Wr, L0_ffn_aux_keys, L0_ffn_aux_values, L0_ffn_Wvd, L0_ffn_Wvu, L0_ffn_Wu1, L0_ffn_bu1, L0_ffn_Wu2, L0_ffn_bu2, L0_ffn_gate_w1, L0_ffn_gate_bias, L0_ffn_log_rel):
    import jax
    import jax.numpy as jnp

    def _L0_attn_ref(x, wq, wk, wv, wo):
        import math
        import jax, jax.numpy as jnp
        import numpy as np

        def _rope_tables(T, h, dtype):
            pos = jnp.arange(T, dtype=jnp.float32)
            thetas = 1.0 / 10000.0 ** (jnp.arange(0, h, 2, dtype=jnp.float32) / h)
            pt = jnp.outer(pos, thetas)
            pt = jnp.concatenate([pt, pt], axis=-1)
            return (jnp.sin(pt).astype(dtype), jnp.cos(pt).astype(dtype))

        def _apply_rope(x, sin, cos):
            h = x.shape[-1]
            rot = jnp.concatenate([-x[..., h // 2:], x[..., :h // 2]], axis=-1)
            return x * cos + rot * sin
        B, T, C = x.shape
        n_head = 32
        h = C // n_head

        def proj(w):
            y = jnp.einsum('btc,dc->btd', x, w)
            return y.reshape(B, T, n_head, h).transpose(0, 2, 1, 3)
        q, k, v = (proj(wq), proj(wk), proj(wv))
        sin, cos = _rope_tables(T, h, x.dtype)
        q = _apply_rope(q, sin, cos)
        k = _apply_rope(k, sin, cos)
        scores = jnp.einsum('bnth,bnsh->bnts', q, k) * (1.0 / math.sqrt(h))
        causal = jnp.tril(jnp.ones((T, T), dtype=bool))
        scores = jnp.where(causal, scores, -jnp.inf)
        attn = jax.nn.softmax(scores, axis=-1)
        out = jnp.einsum('bnts,bnsh->bnth', attn, v)
        out = out.transpose(0, 2, 1, 3).reshape(B, T, C)
        return jnp.einsum('btc,dc->btd', out, wo)

    def _L0_xattn_ref(q, k, v, start_pos, mask):
        import math
        import jax, jax.numpy as jnp
        import numpy as np
        N_HEADS = 32
        N_KV_HEADS = 8
        N_REP = N_HEADS // N_KV_HEADS
        HEAD_DIM = 1024 // N_HEADS
        b, s, _ = q.shape
        t = k.shape[1]
        xq = q.reshape(b, s, N_KV_HEADS, N_REP, HEAD_DIM)
        xk = k.reshape(b, t, N_KV_HEADS, HEAD_DIM)
        xv = v.reshape(b, t, N_KV_HEADS, HEAD_DIM)
        scores = jnp.einsum('bsgrd,btgd->bgrst', xq, xk) / math.sqrt(HEAD_DIM)
        scores = scores + mask
        probs = jax.nn.softmax(scores.astype(jnp.float32), axis=-1).astype(q.dtype)
        out = jnp.einsum('bgrst,btgd->bsgrd', probs, xv)
        return out.reshape(b, s, N_HEADS * HEAD_DIM)

    def _L0_ffn_ref(hidden_states, Wq, Wr, aux_keys, aux_values, Wvd, Wvu, Wu1, bu1, Wu2, bu2, gate_w1, gate_bias, log_rel):
        import jax, jax.numpy as jnp
        import numpy as np
        HID, BOT, RDIM, NSLOT, K, VB = (1024, 64, 48, 256, 8, 64)
        TAU_LOW, TAU_HIGH, EARLY_EXIT = (0.5, 2.0, 0.05)

        def _uncertainty(h, Wu1, bu1, Wu2, bu2):
            var = jnp.var(h, axis=-1)
            log_var = jnp.log1p(var)
            norm_var = log_var / (jnp.mean(log_var) + 1e-06)
            learned = (jax.nn.gelu(h @ Wu1.T + bu1) @ Wu2.T + bu2)[..., 0]
            return jnp.clip(norm_var * 0.5 + jax.nn.sigmoid(learned) * 2.5, 0.0, 5.0)
        query = hidden_states @ Wq.T
        rq = query @ Wr.T
        rk = aux_keys @ Wr.T
        router_scores = jnp.einsum('bsr,nr->bsn', rq, rk) / np.sqrt(RDIM) + log_rel
        top_scores, top_idx = jax.lax.top_k(router_scores, K)
        sel_keys = aux_keys[top_idx]
        attn = jnp.einsum('bsd,bskd->bsk', query, sel_keys) / np.sqrt(BOT) + log_rel[top_idx]
        w = jax.nn.softmax(attn, axis=-1)
        sel_vals = aux_values[top_idx]
        aux_out = jnp.einsum('bsk,bskh->bsh', w, sel_vals)
        aux_out = aux_out @ Wvd.T @ Wvu.T
        u = _uncertainty(hidden_states, Wu1, bu1, Wu2, bu2)
        u_norm = jnp.clip((u - TAU_LOW) / (TAU_HIGH - TAU_LOW), 0.0, 1.0)
        gate = jax.nn.sigmoid(gate_w1 * u_norm + gate_bias)
        gate = jnp.where(gate < EARLY_EXIT, 0.0, gate)
        return hidden_states + gate[..., None] * aux_out
    x = x + _L0_attn_ref(_layernorm(x, axis=-1), L0_attn_wq, L0_attn_wk, L0_attn_wv, L0_attn_wo)
    x = x + _L0_xattn_ref(_layernorm(x, axis=-1), ctx_1024, ctx_1024, 0, mask_SxS2_ff0)
    x = x + _L0_ffn_ref(_layernorm(x, axis=-1), L0_ffn_Wq, L0_ffn_Wr, L0_ffn_aux_keys, L0_ffn_aux_values, L0_ffn_Wvd, L0_ffn_Wvu, L0_ffn_Wu1, L0_ffn_bu1, L0_ffn_Wu2, L0_ffn_bu2, L0_ffn_gate_w1, L0_ffn_gate_bias, L0_ffn_log_rel)
    return x

_drawn_inputs = setup_inputs


def setup_inputs(seed=0):
    import zlib

    import numpy as np

    out = dict(_drawn_inputs(seed))
    spreads = {'mask_SxS2_ff0': (0.0, 2.0), 'L0_ffn_bu1': (0.0, 2.0), 'L0_ffn_log_rel': (0.0, 2.0)}
    factors = {'L0_ffn_Wq': 61.261,
     'L0_ffn_Wr': 64.0,
     'L0_ffn_aux_keys': 60.262,
     'L0_ffn_aux_values': 60.234,
     'L0_ffn_Wvd': 60.759,
     'L0_ffn_Wvu': 59.804,
     'L0_ffn_Wu1': 64.0,
     'L0_ffn_Wu2': 64.0}
    for name, (base, spread) in spreads.items():
        noise = np.random.default_rng([zlib.crc32(name.encode()), seed]).standard_normal(out[name].shape)
        drawn = base * np.exp(spread * noise) if base else spread * noise
        out[name] = jnp.asarray(drawn.astype(out[name].dtype))
    for name, factor in factors.items():
        out[name] = (out[name] * factor).astype(out[name].dtype)
    return out
```

```python
from contextlib import ExitStack

import concourse.bass as bass
from concourse import mybir
from concourse.alu_op_type import AluOpType as ALU

F32 = mybir.dt.float32
F32R = mybir.dt.float32r
ACT = mybir.ActivationFunctionType
AX = mybir.AxisListType

P = 128
B, S, C = 4, 512, 1024
H, D = 32, 32
G = 8
R = H // G
TOK = B * S
NT = TOK // P
QT = S // P
CC = C // P
KEYS = 1601
KP = 1608
KC = (KP + P - 1) // P
KLAST = KP - (KC - 1) * P
KQ = KP // 4
EPS = 1e-5
BIG = 1e38
ITS = B * G
NS, BOT, RD, HU = 256, 64, 48, 256


class Chain:

    def __init__(self, eng, sem):
        self.eng, self.sem, self.base, self.n = eng, sem, 0, 0

    def __call__(self, ins):
        ins.then_inc(self.sem, 1)
        self.n += 1
        self.eng.wait_ge(self.sem, self.base + self.n)


class Kit:

    def __init__(self, nc, name):
        self.nc, self.name, self.ctx = nc, name, ExitStack()

    def sb(self, name, shape, dt=F32):
        return self.ctx.enter_context(self.nc.sbuf_tensor(f"{self.name}_{name}", shape, dt))

    def ps(self, name, shape, dt=F32):
        return self.ctx.enter_context(self.nc.psum_tensor(f"{self.name}_{name}", shape, dt))


def semaphores(nc, keep, stage, names):
    return [keep.enter_context(nc.semaphore(f"{stage}_{n}")) for n in names.split()]


def stage_a(nc, keep, passed, x, wqkvT, rope, ident_d, qk_hi, qk_lo, v_dram):
    HT = NT // 2
    HTOK = HT * P
    NJ = 6
    NR = 4
    PARTS = 4
    PC = CC // PARTS
    STEPS = 2 * NJ
    SLOTS = [(J, t) for J in range(STEPS) for t in range(HT)]
    k = Kit(nc, "a")
    (x_in0, x_in1, var_ready, rstd_ready, xn_ready, xt_ready, xhi_ready, xlo_ready, chain_s, const_in,
     w_in0, w_in1, w_in2, w_in3, whi_ready, wlo_ready, mm_done, ab_ready, roped, rt_ready, shi_ready, slo_ready,
     st_out0, st_out1, v_ready, v_out0, v_out1, expo_ready) = semaphores(
        nc, keep, "a", "x_in0 x_in1 var_ready rstd_ready xn_ready xt_ready xhi_ready xlo_ready chain const_in "
        "w_in0 w_in1 w_in2 w_in3 whi_ready wlo_ready mm_done ab_ready roped rt_ready shi_ready slo_ready "
        "st_out0 st_out1 v_ready v_out0 v_out1 expo_ready")
    x_in, st_out, v_out, w_in = [x_in0, x_in1], [st_out0, st_out1], [v_out0, v_out1], [w_in0, w_in1, w_in2, w_in3]

    def tiles_before(J, t, roped_):
        return sum((j % NJ < NR) == roped_ for j, m in SLOTS[:J * HT + t])

    def rope_tile(J, t):
        return tiles_before(J, t, True) if J % NJ < NR else None

    def behind(J, t):
        if J * HT + t == 0:
            return None
        j, m = SLOTS[J * HT + t - 1]
        r = rope_tile(j, m)
        return None if r is None else (j, m, r)

    def norm_in(J, t):
        if J == 0 and t + 2 < HT:
            return t + 2
        if J == NJ - 1:
            return HT + t
        return None

    with k.ctx:
        ident = k.sb("ident", [P, P])
        rope_sb = k.sb("rope", [P, 2, 2, QT, D])
        xb = k.sb("x", [P, 2, C])
        xn = k.sb("xn", [P, 2, C])
        stats = k.sb("stats", [P, 2, 6])
        mv = k.sb("mv", [P, 2, 2])
        veps = k.sb("veps", [P, 2])
        rstd = k.sb("rstd", [P, 2])
        expo = k.sb("expo", [P, 1])
        XH = k.sb("XH", [P, CC, HTOK], F32R)
        XL = k.sb("XL", [P, CC, HTOK], F32R)
        wraw = k.sb("wraw", [P, CC, 512])
        WH = k.sb("WH", [P, 2, CC, 512], F32R)
        WL = k.sb("WL", [P, 2, CC, 512], F32R)
        qcos = k.sb("qcos", [P, 2, 512])
        qsin = k.sb("qsin", [P, 2, 512])
        qr = k.sb("qr", [P, 2, 512])
        st_hi = k.sb("st_hi", [P, 2, 4, P], F32R)
        st_lo = k.sb("st_lo", [P, 2, 4, P], F32R)
        vst = k.sb("vst", [P, 2, 512])
        Tx = k.ps("Tx", [P, CC, P])
        T = k.ps("T", [P, 2, 4, P])
        M = k.ps("M", [P, 4, 512])
        block = k.ctx.enter_context(nc.Block())

        @block.sync
        def _(sp):
            def load_x(u):
                wait(sp, xn_ready, u - 1)
                sp.dma_start(xb[:, u % 2, :], x[u * P:(u + 1) * P, :]).then_inc(x_in[u % 2], 16)

            def load_w(J):
                for p in range(PARTS):
                    wait(sp, whi_ready, (J - 1) * PARTS + p + 1)
                    wait(sp, wlo_ready, (J - 1) * PARTS + p + 1)
                    rows = slice(p * PC * P, (p + 1) * PC * P)
                    sp.dma_start(wraw[:, p * PC:(p + 1) * PC, :],
                                 wqkvT[rows, (J % NJ) * 512:(J % NJ + 1) * 512]
                                 .rearrange("(c p) n -> p c n", p=P)).then_inc(w_in[p], 16)

            def store(J, t):
                h, j = J // NJ, J % NJ
                b = h * 2 + t // QT
                if j < NR:
                    kq, cols, r = j // 2, (j % 2) * 512, rope_tile(J, t)
                    row = (kq * B + b) * C + cols
                    for ready, buf, dst in ((shi_ready, st_hi, qk_hi), (slo_ready, st_lo, qk_lo)):
                        sp.wait_ge(ready, r + 1)
                        sp.dma_start(dst[row:row + 512, (t % QT) * P:(t % QT + 1) * P]
                                     .rearrange("(c p) t -> p c t", p=P),
                                     buf[:, r % 2, :, :].bitcast(F32)).then_inc(st_out[r % 2], 16)
                else:
                    n = tiles_before(J, t, False)
                    sp.wait_ge(v_ready, n + 1)
                    row = (b * G + (j - NR) * 4) * S
                    sp.dma_start(v_dram[row:row + 4 * S, :].rearrange("(g q p) c -> q p g c", q=QT, p=P)[t % QT],
                                 vst[:, n % 2, :].rearrange("p (g c) -> p g c", g=4)).then_inc(v_out[n % 2], 16)

            load_x(0)
            sp.dma_start(ident[:, :], ident_d).then_inc(const_in, 16)
            load_x(1)
            sp.dma_start(rope_sb[:, :, :, :, :], rope).then_inc(const_in, 16)
            load_w(0)
            for n, (J, t) in enumerate(SLOTS):
                u = norm_in(J, t)
                if u is not None and u < HT:
                    load_x(u)
                if J == NJ - 1 and t == 0:
                    load_x(HT)
                if J == NJ - 1 and t + 1 < HT:
                    load_x(HT + t + 1)
                if n == 0:
                    load_w(1)
                if t == 5 and J + 2 < STEPS:
                    load_w(J + 2)
                if n >= 2:
                    store(*SLOTS[n - 2])
            store(*SLOTS[-2])
            store(*SLOTS[-1])
            for s in range(2):
                sp.wait_ge(st_out[s], 2 * NR * HT * 16)
                sp.wait_ge(v_out[s], (NJ - NR) * HT * 16)

        @block.gpsimd
        def _(pool):
            def power(u):
                pool.wait_ge(var_ready, u + 1)
                nc.gpsimd.tensor_tensor(out=rstd[:, u % 2:u % 2 + 1], in0=veps[:, u % 2:u % 2 + 1],
                                        in1=expo[:, :], op=ALU.pow).then_inc(rstd_ready, 1)

            pool.memset(expo[:, :], -0.5).then_inc(expo_ready, 1)
            pool.wait_ge(expo_ready, 1)
            power(0)
            power(1)
            for J, t in SLOTS:
                u = norm_in(J, t)
                if u is not None:
                    power(u)
                r = rope_tile(J, t)
                if r is not None:
                    pool.wait_ge(ab_ready, r + 1)
                    wait(pool, rt_ready, r - 1)
                    nc.gpsimd.tensor_tensor(out=qr[:, r % 2, :], in0=qcos[:, r % 2, :],
                                            in1=qsin[:, r % 2, :], op=ALU.add).then_inc(roped, 1)

        @block.scalar
        def _(act):
            def split_w(J):
                for p in range(PARTS):
                    act.wait_ge(w_in[p], (J + 1) * 16)
                    wait(act, mm_done, (J - 1) * HT)
                    nc.scalar.activation(WH[:, J % 2, p * PC:(p + 1) * PC, :], wraw[:, p * PC:(p + 1) * PC, :],
                                         ACT.Copy).then_inc(whi_ready, 1)

            def xhi(u):
                act.wait_ge(xt_ready, u + 1)
                if u >= HT:
                    act.wait_ge(mm_done, (NJ - 1) * HT + u - HT + 1)
                nc.scalar.activation(XH[:, :, (u % HT) * P:(u % HT + 1) * P], Tx[:, :, :],
                                     ACT.Copy).then_inc(xhi_ready, 1)

            def shi(r):
                act.wait_ge(rt_ready, r + 1)
                wait(act, st_out[r % 2], r // 2 * 32)
                nc.scalar.activation(st_hi[:, r % 2, :, :], T[:, r % 2, :, :], ACT.Copy).then_inc(shi_ready, 1)

            xhi(0)
            xhi(1)
            split_w(0)
            for J, t in SLOTS:
                u = norm_in(J, t)
                if u is not None:
                    xhi(u)
                before = behind(J, t)
                if before:
                    shi(before[2])
                if J == 0 and t == 2:
                    split_w(1)
                if t == HT - 1 and J + 2 < STEPS:
                    split_w(J + 2)

        @block.vector
        def _(dve):
            chain = Chain(dve, chain_s)

            def split_w(J):
                for p in range(PARTS):
                    dve.wait_ge(whi_ready, J * PARTS + p + 1)
                    nc.vector.tensor_tensor(out=WL[:, J % 2, p * PC:(p + 1) * PC, :],
                                            in0=wraw[:, p * PC:(p + 1) * PC, :],
                                            in1=WH[:, J % 2, p * PC:(p + 1) * PC, :].bitcast(F32),
                                            op=ALU.subtract).then_inc(wlo_ready, 1)

            def norm(u):
                s = u % 2
                dve.wait_ge(x_in[s], (u // 2 + 1) * 16)
                nc.vector.bn_stats(stats[:, 0, :], xb[:, s, 0:512])
                chain(nc.vector.bn_stats(stats[:, 1, :], xb[:, s, 512:1024]))
                chain(nc.vector.bn_aggr(mv[:, s, :], stats[:, :, :]))
                nc.vector.tensor_scalar(out=veps[:, s:s + 1], in0=mv[:, s, 1:2], scalar1=EPS, scalar2=None,
                                        op0=ALU.add).then_inc(var_ready, 1)
                dve.wait_ge(rstd_ready, u + 1)
                wait(dve, xt_ready, u - 1)
                nc.vector.tensor_scalar(out=xn[:, s, :], in0=xb[:, s, :], scalar1=mv[:, s, 0:1],
                                        scalar2=rstd[:, s:s + 1], op0=ALU.subtract,
                                        op1=ALU.mult).then_inc(xn_ready, 1)

            def xlo(u):
                dve.wait_ge(xhi_ready, u + 1)
                cols = slice((u % HT) * P, (u % HT + 1) * P)
                nc.vector.tensor_tensor(out=XL[:, :, cols], in0=Tx[:, :, :], in1=XH[:, :, cols].bitcast(F32),
                                        op=ALU.subtract).then_inc(xlo_ready, 1)

            def rotate(J, t, r):
                s, kq = r % 2, J % NJ // 2
                wait(dve, roped, r - 1)
                heads = M[:, (J * HT + t) % 4, :].rearrange("p (h d) -> p h d", d=D)
                cos = rope_sb[:, kq, 0, t % QT, :].unsqueeze(1).broadcast_to([P, 16, D])
                sin = rope_sb[:, kq, 1, t % QT, :].unsqueeze(1).broadcast_to([P, 16, D])
                oc = qcos[:, s, :].rearrange("p (h d) -> p h d", d=D)
                os = qsin[:, s, :].rearrange("p (h d) -> p h d", d=D)
                nc.vector.tensor_tensor(out=oc, in0=heads, in1=cos, op=ALU.mult)
                for lo, hi in ((0, 16), (16, 0)):
                    last = nc.vector.tensor_tensor(out=os[:, :, lo:lo + 16], in0=heads[:, :, hi:hi + 16],
                                                   in1=sin[:, :, lo:lo + 16], op=ALU.mult)
                last.then_inc(ab_ready, 1)

            def slo(r):
                s = r % 2
                dve.wait_ge(shi_ready, r + 1)
                wait(dve, st_out[s], r // 2 * 32)
                nc.vector.tensor_tensor(out=st_lo[:, s, :, :], in0=T[:, s, :, :],
                                        in1=st_hi[:, s, :, :].bitcast(F32), op=ALU.subtract).then_inc(slo_ready, 1)

            norm(0)
            norm(1)
            xlo(0)
            xlo(1)
            split_w(0)
            dve.wait_ge(const_in, 32)
            for n, (J, t) in enumerate(SLOTS):
                u = norm_in(J, t)
                if u is not None:
                    norm(u)
                r = rope_tile(J, t)
                dve.wait_ge(mm_done, n + 1)
                if r is not None:
                    rotate(J, t, r)
                else:
                    v = tiles_before(J, t, False)
                    wait(dve, v_out[v % 2], v // 2 * 16)
                    nc.vector.tensor_copy(vst[:, v % 2, :], M[:, n % 4, :]).then_inc(v_ready, 1)
                if u is not None:
                    xlo(u)
                before = behind(J, t)
                if before:
                    slo(before[2])
                if J == 0 and t == 2:
                    split_w(1)
                if t == HT - 1 and J + 2 < STEPS:
                    split_w(J + 2)

        @block.tensor
        def _(pe):
            def rows_t(u):
                pe.wait_ge(xn_ready, u + 1)
                wait(pe, xlo_ready, u)
                for c in range(CC):
                    last = nc.tensor.transpose(Tx[:, c, :], xn[:, u % 2, c * P:(c + 1) * P], ident[:, :])
                last.then_inc(xt_ready, 1)

            def heads_t(r):
                pe.wait_ge(roped, r + 1)
                wait(pe, slo_ready, r - 1)
                for c in range(4):
                    last = nc.tensor.transpose(T[:, r % 2, c, :], qr[:, r % 2, c * P:(c + 1) * P], ident[:, :])
                last.then_inc(rt_ready, 1)

            def project(J, t):
                n = J * HT + t
                pe.wait_ge(xhi_ready, J // NJ * HT + t + 1)
                pe.wait_ge(xlo_ready, J // NJ * HT + t + 1)
                if n >= 4:
                    j, m = SLOTS[n - 4]
                    if rope_tile(j, m) is not None:
                        pe.wait_ge(ab_ready, rope_tile(j, m) + 1)
                    else:
                        pe.wait_ge(v_ready, tiles_before(j, m, False) + 1)
                for c in range(CC):
                    if t == 0 and c % PC == 0:
                        pe.wait_ge(whi_ready, J * PARTS + c // PC + 1)
                        pe.wait_ge(wlo_ready, J * PARTS + c // PC + 1)
                    for q, (a, w) in enumerate(((XH, WH), (XL, WH), (XH, WL))):
                        last = nc.tensor.matmul(M[:, n % 4, :], a[:, c, t * P:(t + 1) * P], w[:, J % 2, c, :],
                                                start=c == 0 and q == 0, stop=c == CC - 1 and q == 2)
                last.then_inc(mm_done, 1)

            pe.wait_ge(const_in, 32)
            rows_t(0)
            rows_t(1)
            for J, t in SLOTS:
                project(J, t)
                u = norm_in(J, t)
                if u is not None:
                    rows_t(u)
                before = behind(J, t)
                if before:
                    heads_t(before[2])


def wait(eng, sem, value):
    if not isinstance(value, int) or value > 0:
        eng.wait_ge(sem, value)


def apart(eng, sem):
    eng.sem_inc(sem, 1)


def pairs(eng, body, last):
    for it in (0, 1):
        body(it, it % 2)
    with eng.Fori(1, last // 2) as i:
        for s in (0, 1):
            body(2 * i + s, s)
    for it in (last - 1, last):
        body(it, it % 2)


def stage_b(nc, keep, passed, early, ident_d, causal_d, qk_hi, qk_lo, v_dram, ao_hi, ao_lo):
    NB = R * QT
    LAG = 4
    AHEAD = LAG + 1
    RING = 8
    NLOAD = 8
    SC_BANK = [n % 3 for n in range(NB - 1)] + [1]
    T_BANK = [n % 4 for n in range(NB)]
    VALUES_AT = {1: 0, 3: 1, 5: 2, 7: 3}
    SPREAD_AT = 11
    INVERT_AT, OUT_AT, SCALE_AT = 2, 11, 15
    SPLIT_AT = 3
    ON_ACT = [n for n in range(NB) if n % 4 == 2]
    k = Kit(nc, "b")
    (const_in, in0, in1, v_in0, v_in1, sc_done, mx_done, ex_done, tr_done, ev_act, ev_dve, pv_done, osb_ready, rinv_ready,
     rexp_ready, rb_ready, ao_ready, aoh_ready, aol_ready, out0, out1) = semaphores(
        nc, keep, "b", "const_in in0 in1 v_in0 v_in1 sc_done mx_done ex_done tr_done ev_act ev_dve pv_done osb_ready rinv_ready "
        "rexp_ready rb_ready ao_ready aoh_ready aol_ready out0 out1")
    in_q, v_in, out_q = [in0, in1], [v_in0, v_in1], [out0, out1]

    def evac_done(eng, count):
        it, n = count
        wait(eng, ev_act, it * len(ON_ACT) + sum(m < n for m in ON_ACT))
        wait(eng, ev_dve, it * (NB - len(ON_ACT)) + sum(m < n for m in range(NB) if m not in ON_ACT))

    with k.ctx:
        ident = k.sb("ident", [P, P])
        causal = k.sb("causal", [P, S])
        Q = k.sb("Q", [P, 2, R, S], F32R)
        K = k.sb("K", [P, 2, R, S], F32R)
        V = k.sb("V", [P, 2, QT, P])
        prob = k.sb("prob", [P, RING, S])
        PT = k.sb("PT", [P, 2, R, QT, S])
        nmax = k.sb("nmax", [P, 2, NB])
        rsum = k.sb("rsum", [P, 2, NB])
        rinv = k.sb("rinv", [P, 2, NB])
        rexp = k.sb("rexp", [P, QT, R, D])
        osb = k.sb("osb", [P, S])
        ao = k.sb("ao", [P, S])
        aoh = k.sb("aoh", [P, 2, S], F32R)
        aol = k.sb("aol", [P, 2, S], F32R)
        SC = k.ps("SC", [P, 3, S])
        T = k.ps("T", [P, 4, S])
        O = k.ps("O", [P, S])
        block = k.ctx.enter_context(nc.Block())
        last_it = ITS - 1

        def turn(it, s):
            return it // 2 if isinstance(it, int) else (it - s) // 2

        def before(it, n, banks):
            m = next(m for m in range(n - 1, n - NB - 1, -1) if banks[m % NB] == banks[n])
            return (it, m) if m >= 0 else (it - 1, m + NB)

        def inside(it):
            return not isinstance(it, int) or 0 <= it <= last_it

        def shifted(it, n, s, by):
            n += by
            if 0 <= n < NB:
                return it, n, s
            step = 1 if n >= NB else -1
            return (it + step, n - step * NB, 1 - s) if inside(it + step) else None

        @block.sync
        def _(sp):
            def load(it, s):
                wait(sp, sc_done, (it - 1) * NB)
                for buf, kq, order in ((Q, 0, (qk_hi, qk_hi, qk_lo, qk_lo)), (K, 1, (qk_hi, qk_lo, qk_hi, qk_lo))):
                    for r, src in enumerate(order):
                        sp.dma_start(buf[32 * r:32 * r + 32, s, :, :].bitcast(F32),
                                     src[bass.ds(kq * B * C + it * P, P), :]
                                     .rearrange("(j p) t -> p j t", p=D)).then_inc(in_q[s], 16)
                wait(sp, pv_done, it - 1)
                sp.dma_start(V[:, s, :, :], v_dram[bass.ds(it * S, S), :]
                             .rearrange("(k p) d -> p k d", p=P)).then_inc(v_in[s], 16)

            def store(it, s):
                for ready, buf, dst in ((aoh_ready, aoh, ao_hi), (aol_ready, aol, ao_lo)):
                    sp.wait_ge(ready, it + 1)
                    sp.dma_start(dst[bass.ds(it * P, P), :], buf[:, s, :].bitcast(F32)).then_inc(out_q[s], 16)

            def body(it, s):
                if isinstance(it, int) and it == 1:
                    for dst, src, signal in early:
                        sp.dma_start(dst, src).then_inc(signal, 16)
                if not (isinstance(it, int) and it == last_it):
                    load(it + 1, 1 - s)
                if not (isinstance(it, int) and it < 2):
                    store(it - 2, s)

            sp.dma_start(ident[:, :], ident_d).then_inc(const_in, 16)
            sp.dma_start(causal[:, :], causal_d).then_inc(const_in, 16)
            load(0, 0)
            pairs(sp, body, last_it)
            store(last_it - 1, 1 - last_it % 2)
            store(last_it, last_it % 2)
            for s in range(2):
                sp.wait_ge(out_q[s], ITS // 2 * 32)

        @block.gpsimd
        def _(pool):
            def body(it, s):
                pool.wait_ge(rinv_ready, it + 1)
                wait(pool, rb_ready, it)
                apart(pool, passed["pool"])
                nc.gpsimd.tensor_copy(rexp[:, :, :, :], rinv[:, s, :].rearrange("p (j q) -> p q j", q=QT)
                                      .unsqueeze(3).broadcast_to([P, QT, R, D])).then_inc(rexp_ready, 1)
            pairs(pool, body, last_it)

        @block.tensor
        def _(pe):
            def scores(it, n, s):
                j, qt = n // QT, n % QT
                if n == 0:
                    pe.wait_ge(in_q[s], (turn(it, s) + 1) * 16 * NLOAD)
                i, m = before(it, n, SC_BANK)
                wait(pe, mx_done, i * NB + m + 1)
                cols = max((qt + 1) * P, 256)
                nc.tensor.matmul(SC[:, SC_BANK[n], 0:cols], Q[:, s, j, qt * P:(qt + 1) * P], K[:, s, j, 0:cols],
                                 start=True, stop=True).then_inc(sc_done, 1)

            def transposes(it, n, s):
                pe.wait_ge(ex_done, it * NB + n + 1)
                i, m = before(it, n, T_BANK)
                evac_done(pe, (i, m + 1))
                for c in range(n % QT + 1):
                    last = nc.tensor.transpose(T[:, T_BANK[n], c * P:(c + 1) * P], prob[:, n % RING, c * P:(c + 1) * P],
                                               ident[:, :])
                last.then_inc(tr_done, 1)

            def values(it, c, s):
                if c == 0:
                    pe.wait_ge(v_in[s], (turn(it, s) + 1) * 16)
                    evac_done(pe, (it + 1, 0))
                    wait(pe, ao_ready, it)
                for j in range(R):
                    last = nc.tensor.matmul(O[32 * j:32 * j + 32, c * P:S], V[:, s, c, 32 * j:32 * j + 32],
                                            PT[:, s, j, c, c * P:S], start=c == 0, stop=c == QT - 1)
                if c == QT - 1:
                    last.then_inc(pv_done, 1)

            def spread(it):
                pe.wait_ge(rexp_ready, it + 1)
                pe.wait_ge(osb_ready, it + 1)
                for qt in range(QT):
                    last = nc.tensor.transpose(O[:, qt * P:(qt + 1) * P],
                                               rexp[:, qt, :, :].rearrange("p j d -> p (j d)"), ident[:, :])
                last.then_inc(rb_ready, 1)

            def behind(it, n, s):
                if n in VALUES_AT:
                    values(it - 1, VALUES_AT[n], 1 - s)
                if n == SPREAD_AT:
                    spread(it - 1)

            def body(it, s):
                for n in range(NB):
                    ahead = shifted(it, n, s, AHEAD)
                    if ahead:
                        scores(*ahead)
                    transposes(it, n, s)
                    if not (isinstance(it, int) and it == 0):
                        behind(it, n, s)

            pe.wait_ge(const_in, 32)
            for n in range(AHEAD):
                scores(0, n, 0)
            pairs(pe, body, last_it)
            for n in range(NB):
                behind(ITS, n, ITS % 2)

        @block.scalar
        def _(act):
            def exponent(it, n, s):
                act.wait_ge(mx_done, it * NB + n + 1)
                row = prob[:, n % RING, 0:(n % QT + 1) * P]
                nc.scalar.activation(row, row, ACT.Exp,
                                     bias=nmax[:, s, n:n + 1], scale=-1.0,
                                     accum_out=rsum[:, s, n:n + 1]).then_inc(ex_done, 1)

            def evac(it, n, s):
                j, qt = n // QT, n % QT
                if n == ON_ACT[0]:
                    wait(act, pv_done, it - 1)
                act.wait_ge(tr_done, it * NB + n + 1)
                nc.scalar.activation(PT[:, s, j, 0:qt + 1, qt * P:(qt + 1) * P],
                                     T[:, T_BANK[n], 0:(qt + 1) * P].rearrange("p (c t) -> p c t", t=P),
                                     ACT.Copy).then_inc(ev_act, 1)

            def copy_out(it):
                act.wait_ge(pv_done, it + 1)
                wait(act, ao_ready, it)
                nc.scalar.activation(osb[:, :], O[:, :], ACT.Copy).then_inc(osb_ready, 1)

            def split(it, s):
                act.wait_ge(ao_ready, it + 1)
                wait(act, out_q[s], turn(it, s) * 32)
                nc.scalar.activation(aoh[:, s, :], ao[:, :], ACT.Copy).then_inc(aoh_ready, 1)

            def behind(it, n, s):
                old = shifted(it, n, s, -LAG)
                if old and old[1] in ON_ACT and inside(old[0]):
                    evac(*old)
                if n == OUT_AT and inside(it - 1):
                    copy_out(it - 1)
                if n == SPLIT_AT and inside(it - 2):
                    split(it - 2, s)

            def body(it, s):
                for n in range(NB):
                    exponent(it, n, s)
                    behind(it, n, s)

            pairs(act, body, last_it)
            for it in (ITS, ITS + 1):
                for n in range(NB):
                    behind(it, n, it % 2)

        @block.vector
        def _(dve):
            def maxima(it, n, s):
                qt = n % QT
                cols = (qt + 1) * P
                dve.wait_ge(sc_done, it * NB + n + 1)
                wait(dve, tr_done, it * NB + n - RING + 1)
                apart(dve, passed["dve"])
                nc.vector.tensor_tensor_reduce(out=prob[:, n % RING, 0:cols], in0=SC[:, SC_BANK[n], 0:cols],
                                               in1=causal[:, S - cols:S], scale=1.0, scalar=3e38, op0=ALU.add,
                                               op1=ALU.min, accum_out=nmax[:, s, n:n + 1]).then_inc(mx_done, 1)

            def evac(it, n, s):
                j, qt = n // QT, n % QT
                if n == 0:
                    wait(dve, pv_done, it - 1)
                dve.wait_ge(tr_done, it * NB + n + 1)
                nc.vector.tensor_copy(PT[:, s, j, 0:qt + 1, qt * P:(qt + 1) * P],
                                      T[:, T_BANK[n], 0:(qt + 1) * P].rearrange("p (c t) -> p c t", t=P)).then_inc(ev_dve, 1)

            def invert(it, s):
                dve.wait_ge(ex_done, (it + 1) * NB)
                nc.vector.reciprocal(rinv[:, s, :], rsum[:, s, :]).then_inc(rinv_ready, 1)

            def scale(it):
                dve.wait_ge(osb_ready, it + 1)
                dve.wait_ge(rb_ready, it + 1)
                wait(dve, aol_ready, it)
                nc.vector.tensor_tensor(out=ao[:, :], in0=O[:, :], in1=osb[:, :], op=ALU.mult).then_inc(ao_ready, 1)

            def split(it, s):
                dve.wait_ge(aoh_ready, it + 1)
                nc.vector.tensor_tensor(out=aol[:, s, :], in0=ao[:, :], in1=aoh[:, s, :].bitcast(F32),
                                        op=ALU.subtract).then_inc(aol_ready, 1)

            def behind(it, n, s):
                old = shifted(it, n, s, -LAG)
                if old and old[1] not in ON_ACT and inside(old[0]):
                    evac(*old)
                if n == INVERT_AT and inside(it - 1):
                    invert(it - 1, 1 - s)
                if n == SCALE_AT and inside(it - 1):
                    scale(it - 1)
                if n == SPLIT_AT and inside(it - 2):
                    split(it - 2, s)

            def body(it, s):
                for n in range(NB):
                    maxima(it, n, s)
                    behind(it, n, s)

            dve.wait_ge(const_in, 32)
            pairs(dve, body, last_it)
            for it in (ITS, ITS + 1):
                for n in range(NB):
                    behind(it, n, it % 2)


def stage_c(nc, keep, passed, wraw, wo_in, mask, mask_in, x, ident_d, ao_hi, ao_lo, x1, q2_hi, q2_lo):
    k = Kit(nc, "c")
    (const_in, neg_ready, whi_ready, wlo_ready, in0, in1, mm_done, res_ready, chain_s, var_ready, rstd_ready, xn_ready,
     xt_ready, hi_ready, lo_ready, x1_out0, x1_out1, q_out0, q_out1, expo_ready) = semaphores(
        nc, keep, "c", "const_in neg_ready whi_ready wlo_ready in0 in1 mm_done res_ready chain var_ready rstd_ready "
        "xn_ready xt_ready hi_ready lo_ready x1_out0 x1_out1 q_out0 q_out1 expo_ready")
    in_q, x1_out, q_out = [in0, in1], [x1_out0, x1_out1], [q_out0, q_out1]
    NLOAD = 3
    PARTS = 4
    PC = CC // PARTS
    QSCALE = -1.0 / D ** 0.5
    with k.ctx:
        ident = k.sb("ident", [P, P])
        WH = k.sb("WH", [P, 2, CC, 512], F32R)
        WL = k.sb("WL", [P, 2, CC, 512], F32R)
        AH = k.sb("AH", [P, 2, CC, P], F32R)
        AL = k.sb("AL", [P, 2, CC, P], F32R)
        xb = k.sb("x", [P, 2, C])
        res = k.sb("res", [P, 2, C])
        xn = k.sb("xn", [P, C])
        stats = k.sb("stats", [P, 2, 6])
        mv = k.sb("mv", [P, 2])
        veps = k.sb("veps", [P, 1])
        rstd = k.sb("rstd", [P, 1])
        expo = k.sb("expo", [P, 1])
        QH = k.sb("QH", [P, 2, CC, P], F32R)
        QL = k.sb("QL", [P, 2, CC, P], F32R)
        M = k.ps("M", [P, 4, 512])
        T = k.ps("T", [P, 2, CC, P])
        block = k.ctx.enter_context(nc.Block())

        @block.sync
        def _(sp):
            def load(b, qt):
                s = qt % 2
                n = b * QT + qt
                wait(sp, mm_done, 2 * n - 2)
                wait(sp, res_ready, 2 * n - 2)
                for src, dst in ((ao_hi, AH), (ao_lo, AL)):
                    sp.dma_start(dst[:, s, :, :].bitcast(F32),
                                 src[bass.ds(b * C, C), qt * P:(qt + 1) * P]
                                 .rearrange("(c p) t -> p c t", p=P)).then_inc(in_q[s], 16)
                sp.dma_start(xb[:, s, :], x[bass.ds(b * S + qt * P, P), :]).then_inc(in_q[s], 16)

            def store(b, qt):
                s = qt % 2
                n = b * QT + qt
                sp.wait_ge(res_ready, 2 * n + 2)
                sp.dma_start(x1[bass.ds(b * G * S, G * S), :].rearrange("(g q p) c -> q p g c", q=QT, p=P)[qt],
                             res[:, s, :].rearrange("p (g c) -> p g c", g=G)).then_inc(x1_out[s], 16)
                for ready, buf, dst in ((hi_ready, QH, q2_hi), (lo_ready, QL, q2_lo)):
                    sp.wait_ge(ready, n + 1)
                    sp.dma_start(dst[bass.ds(b * C, C), qt * P:(qt + 1) * P].rearrange("(c p) t -> p c t", p=P),
                                 buf[:, s, :, :].bitcast(F32)).then_inc(q_out[s], 16)

            sp.dma_start(ident[:, :], ident_d).then_inc(const_in, 16)
            load(0, 0)
            load(0, 1)
            for qt in range(2):
                load(0, qt + 2)
                store(0, qt)
            with sp.Fori(1, B) as b:
                for qt in range(QT):
                    load(b, qt)
                    store(b - 1, qt + 2) if qt < 2 else store(b, qt - 2)
            store(B - 1, 2)
            store(B - 1, 3)
            for s in range(2):
                sp.wait_ge(x1_out[s], NT // 2 * 16)
                sp.wait_ge(q_out[s], NT // 2 * 32)

        @block.gpsimd
        def _(pool):
            pool.memset(expo[:, :], -0.5).then_inc(expo_ready, 1)
            pool.wait_ge(expo_ready, 1)
            with pool.Fori(0, NT) as t:
                pool.wait_ge(var_ready, t + 1)
                nc.gpsimd.tensor_tensor(out=rstd[:, :], in0=veps[:, :], in1=expo[:, :],
                                        op=ALU.pow).then_inc(rstd_ready, 1)

        @block.scalar
        def _(act):
            act.wait_ge(wo_in, 16)
            for half in range(2):
                for p in range(PARTS):
                    cols = slice(p * PC, (p + 1) * PC)
                    nc.scalar.activation(WH[:, half, cols, :], wraw[:, cols, half * 512:(half + 1) * 512],
                                         ACT.Copy).then_inc(whi_ready, 1)

            def high(b, qt):
                act.wait_ge(xt_ready, b * QT + qt + 1)
                wait(act, q_out[qt % 2], (b * 2 + qt // 2) * 32)
                nc.scalar.activation(QH[:, qt % 2, :, :], T[:, qt % 2, :, :], ACT.Copy,
                                     scale=QSCALE).then_inc(hi_ready, 1)

            for qt in range(QT):
                high(0, qt)
            act.wait_ge(mask_in, 16)
            nc.scalar.activation(mask[:, :, :], mask[:, :, :], ACT.Copy, scale=-1.0).then_inc(neg_ready, 1)
            with act.Fori(1, B) as b:
                for qt in range(QT):
                    high(b, qt)

        @block.vector
        def _(dve):
            for half in range(2):
                for p in range(PARTS):
                    cols = slice(p * PC, (p + 1) * PC)
                    dve.wait_ge(whi_ready, half * PARTS + p + 1)
                    nc.vector.tensor_tensor(out=WL[:, half, cols, :], in0=wraw[:, cols, half * 512:(half + 1) * 512],
                                            in1=WH[:, half, cols, :].bitcast(F32),
                                            op=ALU.subtract).then_inc(wlo_ready, 1)
            chain = Chain(dve, chain_s)

            def low(b, qt):
                dve.wait_ge(hi_ready, b * QT + qt + 1)
                nc.vector.scalar_tensor_tensor(out=QL[:, qt % 2, :, :], in0=T[:, qt % 2, :, :], scalar=QSCALE,
                                               in1=QH[:, qt % 2, :, :].bitcast(F32), op0=ALU.mult,
                                               op1=ALU.subtract).then_inc(lo_ready, 1)

            def batch(b):
                chain.base, chain.n = b * 2 * QT, 0
                for qt in range(QT):
                    s = qt % 2
                    n = b * QT + qt
                    dve.wait_ge(in_q[s], (b * 2 + qt // 2 + 1) * 16 * NLOAD)
                    wait(dve, x1_out[s], (b * 2 + qt // 2) * 16)
                    for half in range(2):
                        cols = slice(half * 512, half * 512 + 512)
                        dve.wait_ge(mm_done, 2 * n + half + 1)
                        nc.vector.tensor_tensor(out=res[:, s, cols], in0=M[:, 2 * s + half, :], in1=xb[:, s, cols],
                                                op=ALU.add).then_inc(res_ready, 1)
                    dve.wait_ge(res_ready, 2 * n + 2)
                    nc.vector.bn_stats(stats[:, 0, :], res[:, s, 0:512])
                    chain(nc.vector.bn_stats(stats[:, 1, :], res[:, s, 512:1024]))
                    apart(dve, passed["dve"])
                    chain(nc.vector.bn_aggr(mv[:, :], stats[:, :, :]))
                    nc.vector.tensor_scalar(out=veps[:, :], in0=mv[:, 1:2], scalar1=EPS, scalar2=None,
                                            op0=ALU.add).then_inc(var_ready, 1)
                    dve.wait_ge(rstd_ready, n + 1)
                    wait(dve, xt_ready, n)
                    nc.vector.tensor_scalar(out=xn[:, :], in0=res[:, s, :], scalar1=mv[:, 0:1], scalar2=rstd[:, :],
                                            op0=ALU.subtract, op1=ALU.mult).then_inc(xn_ready, 1)
                    low(b, qt)

            batch(0)
            with dve.Fori(1, B) as b:
                batch(b)

        @block.tensor
        def _(pe):
            pe.wait_ge(const_in, 16)

            def rows_t(b, qt):
                pe.wait_ge(xn_ready, b * QT + qt + 1)
                wait(pe, lo_ready, b * QT + qt - 1)
                for c in range(CC):
                    last = nc.tensor.transpose(T[:, qt % 2, c, :], xn[:, c * P:(c + 1) * P], ident[:, :])
                last.then_inc(xt_ready, 1)

            def project(b, qt):
                s = qt % 2
                pe.wait_ge(in_q[s], (b * 2 + qt // 2 + 1) * 16 * NLOAD)
                wait(pe, res_ready, 2 * (b * QT + qt) - 2)
                for half in range(2):
                    for c in range(CC):
                        if isinstance(b, int) and b == 0 and qt == 0 and c % PC == 0:
                            pe.wait_ge(whi_ready, half * PARTS + c // PC + 1)
                            pe.wait_ge(wlo_ready, half * PARTS + c // PC + 1)
                        for q, (a, w) in enumerate(((AH, WH), (AL, WH), (AH, WL))):
                            last = nc.tensor.matmul(M[:, 2 * s + half, :], a[:, s, c, :], w[:, half, c, :],
                                                    start=c == 0 and q == 0, stop=c == CC - 1 and q == 2)
                    last.then_inc(mm_done, 1)

            for qt in range(QT):
                project(0, qt)
                if qt:
                    rows_t(0, qt - 1)
            with pe.Fori(1, B) as b:
                for qt in range(QT):
                    project(b, qt)
                    rows_t(b, qt - 1) if qt else rows_t(b - 1, QT - 1)
            rows_t(B - 1, QT - 1)


def stage_d(nc, keep, passed, mask, ident_d, ctxT, ctxV, low_rows, q2_hi, q2_lo, x1, x2):
    NB = R * QT
    AHEAD = 3
    NLOAD = 6
    RING = 8
    FULL = (KC - 1) // 4
    USES = []
    for _qt in range(QT):
        for _j in range(R):
            for _g in range(FULL):
                USES.append((("full", _qt, _j, _g), "dve" if _g == 1 else "act"))
        USES.append((("last", _qt), "act"))
        USES.append((("out", _qt), "dve"))
    ORDER = [u for u, _ in USES]
    TOTAL = {e: sum(x == e for _, x in USES) for e in ("act", "dve")}
    FLUSH = ("flush",)
    k = Kit(nc, "d")
    (const_in, in0, in1, kraw_in, kraw_hi, k_ready, sc_done, mx_done, ex_done, tr_done, ev_act, ev_dve,
     pv_done, osb_ready, red_ready, rinv_ready, part_ready, sum_ready, out0, out1) = semaphores(
        nc, keep, "d", "const_in in0 in1 kraw_in kraw_hi k_ready sc_done mx_done ex_done tr_done ev_act "
        "ev_dve pv_done osb_ready red_ready rinv_ready part_ready sum_ready out0 out1")
    in_q, out_q = [in0, in1], [out0, out1]
    ev = {"act": ev_act, "dve": ev_dve}

    def count(use, it):
        if use == FLUSH:
            return "dve", ITS * TOTAL["dve"] + 1
        i = ORDER.index(use)
        e = USES[i][1]
        return e, it * TOTAL[e] + sum(x == e for _, x in USES[:i + 1])

    def filled(use, it):
        return it * len(USES) + (1 if use == FLUSH else ORDER.index(use) + 1)

    def slot_of(use):
        return 0 if use == FLUSH else ORDER.index(use) % 3

    def before(use, it):
        i = 0 if use == FLUSH else ORDER.index(use)
        if i >= 3:
            return ORDER[i - 3], it
        return [u for m, u in enumerate(ORDER) if m % 3 == i][-1], it - 1

    with k.ctx:
        ident = k.sb("ident", [P, P])
        lows = k.sb("lows", [P, 1])
        Q = k.sb("Q", [P, 2, R, S], F32R)
        kraw = k.sb("kraw", [P, KP])
        K = k.sb("K", [P, 2, KP], F32R)
        V = k.sb("V", [P, 2, KC, D])
        x1b = k.sb("x1", [P, 2, QT, P])
        res = k.sb("res", [P, 2, QT, P])
        prob = k.sb("prob", [P, RING, KP])
        PT = k.sb("PT", [P, 2, KC, R * P])
        nmax = k.sb("nmax", [P, 2, 2, NB])
        rsum = k.sb("rsum", [P, 2, NB])
        rinv = k.sb("rinv", [P, 2, R])
        osb = k.sb("osb", [P, R * P])
        red = k.sb("red", [P, R, D])
        part = k.sb("part", [P, 2, R, D])
        SC = k.ps("SC", [P, 2, 2, 512])
        T = k.ps("T", [P, 3, 512])
        O = k.ps("O", [P, R * P])
        block = k.ctx.enter_context(nc.Block())
        last_it = ITS - 1

        def turn(it, s):
            return it // 2 if isinstance(it, int) else (it - s) // 2

        @block.sync
        def _(sp):
            def load(it, s):
                wait(sp, k_ready, it)
                for r in range(4):
                    sp.dma_start(kraw[32 * r:32 * r + 32, :], ctxT[bass.ds(it * D, D), :]).then_inc(kraw_in, 16)
                wait(sp, sc_done, (it - 1) * NB * 2)
                apart(sp, passed["sp"])
                wait(sp, pv_done, (it - 1) * QT)
                wait(sp, sum_ready, (it - 1) * QT)
                for r, src in enumerate((q2_hi, q2_hi, q2_lo, q2_lo)):
                    sp.dma_start(Q[32 * r:32 * r + 32, s, :, :].bitcast(F32),
                                 src[bass.ds(it * P, P), :].rearrange("(j p) t -> p j t", p=D)).then_inc(in_q[s], 16)
                sp.dma_start(V[:, s, :, :], ctxV[bass.ds(it * P, P), :, :]).then_inc(in_q[s], 16)
                sp.dma_start(x1b[:, s, :, :], x1[bass.ds(it * S, S), :]
                             .rearrange("(q p) c -> p q c", p=P)).then_inc(in_q[s], 16)

            def store(it, s):
                sp.wait_ge(sum_ready, (it + 1) * QT)
                sp.dma_start(x2[bass.ds(it * S, S), :].rearrange("(q p) c -> p q c", p=P),
                             res[:, s, :, :]).then_inc(out_q[s], 16)

            def body(it, s):
                if not (isinstance(it, int) and it == last_it):
                    load(it + 1, 1 - s)
                if not (isinstance(it, int) and it == 0):
                    store(it - 1, 1 - s)

            sp.dma_start(ident[:, :], ident_d).then_inc(const_in, 16)
            sp.dma_start(lows[:, :], low_rows).then_inc(const_in, 16)
            load(0, 0)
            pairs(sp, body, last_it)
            store(last_it, last_it % 2)
            for s in range(2):
                sp.wait_ge(out_q[s], ITS // 2 * 16)

        @block.gpsimd
        def _(pool):
            def add(it, qt, s):
                if qt == 0:
                    wait(pool, out_q[s], turn(it, s) * 16)
                    pool.wait_ge(in_q[s], (turn(it, s) + 1) * 16 * NLOAD)
                pool.wait_ge(part_ready, it * QT + qt + 1)
                nc.gpsimd.tensor_tensor(out=res[:, s, qt, :], in0=part[:, qt % 2, :, :].rearrange("p j d -> p (j d)"),
                                        in1=x1b[:, s, qt, :], op=ALU.add).then_inc(sum_ready, 1)

            def body(it, s):
                for qt in range(QT):
                    add(it, qt, s)

            pairs(pool, body, last_it)

        @block.tensor
        def _(pe):
            def scores(it, n, s, half):
                if n == 0 and half == 0:
                    pe.wait_ge(in_q[s], (turn(it, s) + 1) * 16 * NLOAD)
                    pe.wait_ge(k_ready, it + 1)
                qt, j = n // R, n % R
                wait(pe, mx_done, (it * NB + n) * 2 + half - 1)
                for c in range(2):
                    part_ = half * 2 + c
                    last = nc.tensor.matmul(SC[:, half, c, 0:KQ], Q[:, s, j, qt * P:(qt + 1) * P],
                                            K[:, s, part_ * KQ:(part_ + 1) * KQ], start=True, stop=True)
                last.then_inc(sc_done, 1)

            def bank(use, it):
                u, i = before(use, it)
                e, c = count(u, i)
                wait(pe, ev[e], c)
                return slot_of(use)

            def transposes(it, n, g):
                qt, j = n // R, n % R
                if g == 0:
                    pe.wait_ge(ex_done, it * NB + n + 1)
                b = bank(("full", qt, j, g), it)
                for c in range(4):
                    last = nc.tensor.transpose(T[:, b, c * P:(c + 1) * P],
                                               prob[:, n % RING, (4 * g + c) * P:(4 * g + c + 1) * P], ident[:, :])
                last.then_inc(tr_done, 1)

            def last_chunk(it, qt):
                b = bank(("last", qt), it)
                for j in range(R):
                    last = nc.tensor.transpose(T[0:KLAST, b, j * P:(j + 1) * P],
                                               prob[:, (qt * R + j) % RING, (KC - 1) * P:KP], ident[:, :])
                last.then_inc(tr_done, 1)

            def values(it, qt, s, r):
                if r == 0:
                    for use in (("full", qt, R - 1, 2), ("last", qt)):
                        e, c = count(use, it)
                        wait(pe, ev[e], c)
                    wait(pe, osb_ready, it * QT + qt)
                for c in range(4):
                    tile = slice(32 * c, 32 * c + 32)
                    if r < 3:
                        nc.tensor.matmul(O[tile, :], V[:, s, 4 * r + c, :], PT[:, qt % 2, 4 * r + c, :],
                                         start=r == 0, stop=False)
                    else:
                        cols = slice(c * P, (c + 1) * P)
                        last = nc.tensor.matmul(O[tile, cols], V[0:KLAST, s, KC - 1, :],
                                                PT[0:KLAST, qt % 2, KC - 1, cols], start=False, stop=True)
                if r == 3:
                    last.then_inc(pv_done, 1)

            def way_out(it, qt, at, at_it):
                b = bank(at, at_it)
                pe.wait_ge(osb_ready, it * QT + qt + 1)
                for j in range(R):
                    last = nc.tensor.transpose(T[:, b, j * P:(j + 1) * P], osb[:, j * P:(j + 1) * P], ident[:, :])
                last.then_inc(tr_done, 1)

            def body(it, s):
                for n in range(NB):
                    qt, j = n // R, n % R
                    ahead = n + AHEAD
                    for half in range(2):
                        if ahead < NB:
                            scores(it, ahead, s, half)
                        elif not (isinstance(it, int) and it == last_it):
                            scores(it + 1, ahead - NB, 1 - s, half)
                        if half == 0:
                            transposes(it, n, 0)
                            transposes(it, n, 1)
                    transposes(it, n, 2)
                    prev = (it, qt - 1, s) if qt else (it - 1, QT - 1, 1 - s)
                    none = isinstance(it, int) and it == 0 and qt == 0
                    if not none and j < 3:
                        values(*prev, j)
                        if j == 2:
                            values(*prev, 3)
                    if j == R - 1:
                        last_chunk(it, qt)
                        if none:
                            b = bank(("out", 0), 0)
                            for m in range(R):
                                last = nc.tensor.transpose(T[:, b, m * P:(m + 1) * P], prob[:, m, 0:P], ident[:, :])
                            last.then_inc(tr_done, 1)
                        else:
                            way_out(prev[0], prev[1], ("out", qt), it)

            pe.wait_ge(const_in, 32)
            for n in range(AHEAD):
                for half in range(2):
                    scores(0, n, 0, half)
            pairs(pe, body, last_it)
            for r in range(4):
                values(last_it, QT - 1, last_it % 2, r)
            way_out(last_it, QT - 1, FLUSH, ITS)

        @block.scalar
        def _(act):
            def exponent(it, n, s):
                act.wait_ge(mx_done, (it * NB + n + 1) * 2)
                nc.scalar.activation(prob[:, n % RING, :], prob[:, n % RING, :], ACT.Exp,
                                     bias=nmax[:, s, 1, n:n + 1], scale=-1.0,
                                     accum_out=rsum[:, s, n:n + 1]).then_inc(ex_done, 1)

            def evac(it, n, g):
                qt, j = n // R, n % R
                use = ("full", qt, j, g)
                if j == 0 and g == 0:
                    wait(act, pv_done, it * QT + qt - 1)
                act.wait_ge(tr_done, filled(use, it))
                nc.scalar.activation(PT[:, qt % 2, 4 * g:4 * g + 4, j * P:(j + 1) * P],
                                     T[:, slot_of(use), :].rearrange("p (c t) -> p c t", t=P),
                                     ACT.Copy).then_inc(ev_act, 1)

            def evac_last(it, qt):
                act.wait_ge(tr_done, filled(("last", qt), it))
                nc.scalar.activation(PT[0:KLAST, qt % 2, KC - 1, :], T[0:KLAST, slot_of(("last", qt)), :],
                                     ACT.Copy).then_inc(ev_act, 1)

            def copy_out(it, qt):
                act.wait_ge(pv_done, it * QT + qt + 1)
                wait(act, tr_done, filled(("out", qt), it))
                nc.scalar.activation(osb[:, :], O[:, :], ACT.Copy).then_inc(osb_ready, 1)

            def split_keys(it, s):
                act.wait_ge(kraw_in, (it + 1) * 64)
                wait(act, sc_done, (it - 1) * NB * 2)
                nc.scalar.activation(K[:, s, :], kraw[:, :], ACT.Copy).then_inc(kraw_hi, 1)

            def body(it, s):
                last = isinstance(it, int) and it == last_it
                for n in range(NB):
                    qt, j = n // R, n % R
                    if n + 1 < NB:
                        exponent(it, n + 1, s)
                    elif not last:
                        exponent(it + 1, 0, 1 - s)
                    evac(it, n, 0)
                    if j == R - 1 and not (isinstance(it, int) and it == 0 and qt == 0):
                        copy_out(*((it, qt - 1) if qt else (it - 1, QT - 1)))
                    evac(it, n, 2)
                    if j == R - 1:
                        evac_last(it, qt)
                    if n == 5 and not last:
                        split_keys(it + 1, 1 - s)

            act.wait_ge(const_in, 32)
            split_keys(0, 0)
            exponent(0, 0, 0)
            pairs(act, body, last_it)
            copy_out(last_it, QT - 1)

        @block.vector
        def _(dve):
            def maxima(it, n, s, half):
                qt = n // R
                m = (it * NB + n) * 2 + half
                dve.wait_ge(sc_done, m + 1)
                if half == 0:
                    unit, j = n // R, n % R
                    u = ("last", unit - 2) if unit >= 2 else ("last", unit + 2)
                    i = it if unit >= 2 else it - 1
                    wait(dve, tr_done, filled(u, i))
                    start = 3e38
                else:
                    dve.wait_ge(mx_done, m)
                    start = nmax[:, s, 0, n:n + 1]
                cols = slice(half * 2 * KQ, (half + 1) * 2 * KQ)
                apart(dve, passed["dve"])
                nc.vector.tensor_tensor_reduce(
                    out=prob[:, n % RING, cols].rearrange("p (c k) -> p c k", k=KQ), in0=SC[:, half, :, 0:KQ],
                    in1=mask[:, qt, cols].rearrange("p (c k) -> p c k", k=KQ), scale=1.0, scalar=start,
                    op0=ALU.add, op1=ALU.min, accum_out=nmax[:, s, half, n:n + 1]).then_inc(mx_done, 1)

            def evac(it, use):
                _, qt, j, g = use
                dve.wait_ge(tr_done, filled(use, it))
                if j == 0:
                    wait(dve, pv_done, it * QT + qt - 1)
                nc.vector.tensor_copy(PT[:, qt % 2, 4 * g:4 * g + 4, j * P:(j + 1) * P],
                                      T[:, slot_of(use), :].rearrange("p (c t) -> p c t", t=P)).then_inc(ev_dve, 1)

            def finish(it, qt, s, use, at_it):
                dve.wait_ge(tr_done, filled(use, at_it))
                n = it * QT + qt
                wait(dve, part_ready, n)
                nc.vector.tensor_reduce(out=red[:, :, :], in_=T[:, slot_of(use), :]
                                        .rearrange("p (j k d) -> p j d k", j=R, k=4), axis=AX.X,
                                        op=ALU.add).then_inc(ev_dve, 1)
                nc.vector.reciprocal(rinv[:, qt % 2, :], rsum[:, s, qt * R:(qt + 1) * R]).then_inc(rinv_ready, 1)
                dve.wait_ge(ev_dve, count(use, at_it)[1])
                dve.wait_ge(rinv_ready, n + 1)
                wait(dve, sum_ready, n - 1)
                nc.vector.tensor_tensor(out=part[:, qt % 2, :, :], in0=red[:, :, :],
                                        in1=rinv[:, qt % 2, :].unsqueeze(2).broadcast_to([P, R, D]),
                                        op=ALU.mult).then_inc(part_ready, 1)

            def split_keys(it, s):
                dve.wait_ge(kraw_hi, it + 1)
                nc.vector.scalar_tensor_tensor(out=K[:, s, :], in0=K[:, s, :].bitcast(F32), scalar=lows[:, :],
                                               in1=kraw[:, :], op0=ALU.mult, op1=ALU.add).then_inc(k_ready, 1)

            def body(it, s):
                last = isinstance(it, int) and it == last_it
                for n in range(NB):
                    qt, j = n // R, n % R
                    ahead = n + AHEAD
                    for half in range(2):
                        if ahead < NB:
                            maxima(it, ahead, s, half)
                        elif not last:
                            maxima(it + 1, ahead - NB, 1 - s, half)
                        if half == 0:
                            evac(it, ("full", qt, j, 1))
                    if j == R - 1:
                        if isinstance(it, int) and it == 0 and qt == 0:
                            dve.wait_ge(tr_done, filled(("out", 0), 0))
                            nc.vector.tensor_copy(osb0[:, :], T[:, slot_of(("out", 0)), 0:1]).then_inc(ev_dve, 1)
                        elif qt:
                            finish(it, qt - 1, s, ("out", qt), it)
                        else:
                            finish(it - 1, QT - 1, 1 - s, ("out", 0), it)
                    if n == 6 and not last:
                        split_keys(it + 1, 1 - s)

            osb0 = red[:, 0, 0:1]
            dve.wait_ge(const_in, 32)
            split_keys(0, 0)
            for n in range(AHEAD):
                for half in range(2):
                    maxima(0, n, 0, half)
            pairs(dve, body, last_it)
            finish(last_it, QT - 1, last_it % 2, FLUSH, ITS)


def stage_e(nc, keep, passed, ident_d, w1_d, wrT_d, keysT_d, avT_d, wvdT_d, wvuT_d, vecs_d, scal_d, x2, out):
    N1 = BOT + HU
    outer = Kit(nc, "e")
    (const_in, in0, in1, in2, in3, chain_s, var_ready, rstd_ready, hn_ready, xt_ready, ht_ready, um_ready, sum_ready,
     q_ready, qt_done, qt_ready, cube_ready, tanh_ready, learn_ready, expo_ready, rk_done, rk_ready, av_done,
     av_ready) = semaphores(
        nc, keep, "e", "const_in in0 in1 in2 in3 chain var_ready rstd_ready hn_ready xt_ready ht_ready um_ready "
        "sum_ready q_ready qt_done qt_ready cube_ready tanh_ready learn_ready expo_ready rk_done rk_ready av_done "
        "av_ready")
    in_q = [in0, in1, in2, in3]
    FRONT, BACK = 3, 5
    NCONST = 9
    last_t = NT - 1
    with outer.ctx:
        ident = outer.sb("ident", [P, P])
        X2 = outer.sb("X2", [P, NT, C])
        keysT = outer.sb("keysT", [BOT, NS])
        wrT = outer.sb("wrT", [BOT, RD])
        rkT = outer.sb("rkT", [RD, NS])
        AV = outer.sb("AV", [P, 2, BOT])
        wvuT = outer.sb("wvuT", [BOT, C])
        vecs = outer.sb("vecs", [P, 3, NS])
        scal = outer.sb("scal", [P, 3])
        QT_ = outer.sb("QT", [BOT, TOK])
        varh = outer.sb("varh", [P, NT])
        learn = outer.sb("learn", [P, NT])
        log_rel, bu1, wu2 = vecs[:, 0, :], vecs[:, 1, :], vecs[:, 2, :]

        k = Kit(nc, "e1")
        with k.ctx:
            w1 = k.sb("w1", [P, CC, N1])
            avT = k.sb("avT", [P, CC, NS])
            wvdT = k.sb("wvdT", [P, CC, BOT])
            stats = k.sb("stats", [P, 2, 6])
            mv = k.sb("mv", [P, 2])
            veps = k.sb("veps", [P, 1])
            rstd = k.sb("rstd", [P, 1])
            expo = k.sb("expo", [P, 1])
            hn = k.sb("hn", [P, 2, C])
            hT = k.sb("hT", [P, 2, CC, P])
            qsb = k.sb("qsb", [P, 2, BOT])
            y = k.sb("y", [P, HU])
            y2 = k.sb("y2", [P, HU])
            y3 = k.sb("y3", [P, HU])
            th = k.sb("th", [P, HU])
            lrn = k.sb("lrn", [P, 1])
            T = k.ps("T", [P, 2, CC, P])
            U = k.ps("U", [P, 2, 512])
            QP = k.ps("QP", [P, 512])
            AP_ = k.ps("AVP", [P, 512])
            block = k.ctx.enter_context(nc.Block())

            @block.sync
            def _(sp):
                for dst, src in ((ident, ident_d), (w1, w1_d), (wrT, wrT_d), (keysT, keysT_d), (avT, avT_d),
                                 (wvdT, wvdT_d), (wvuT, wvuT_d)):
                    sp.dma_start(dst[:], src).then_inc(const_in, 16)
                sp.dma_start(vecs[:, :, :].rearrange("p a b -> p (a b)"), vecs_d.partition_broadcast(P)).then_inc(const_in, 16)
                sp.dma_start(scal[:, :], scal_d.partition_broadcast(P)).then_inc(const_in, 16)

                def load(b):
                    for qt in range(QT):
                        wait(sp, in_q[qt], b * 16)
                        sp.dma_start(X2[:, bass.ds(b * QT + qt, 1), :].rearrange("p o (g c) -> p (o g) c", g=G),
                                     x2[bass.ds(b * G * S, G * S), :]
                                     .rearrange("(g q p) c -> q p g c", q=QT, p=P)[qt]).then_inc(in_q[qt], 16)

                load(0)
                with sp.Fori(1, B) as b:
                    load(b)

            def tiles(eng, body):
                for t in range(QT):
                    body(t, t, 0)
                with eng.Fori(1, B) as b:
                    for m in range(QT):
                        body(b * QT + m, m, b)

            @block.gpsimd
            def _(pool):
                pool.memset(expo[:, :], -0.5).then_inc(expo_ready, 1)
                pool.wait_ge(expo_ready, 1)

                def body(t, m, b):
                    pool.wait_ge(var_ready, t + 1)
                    nc.gpsimd.tensor_tensor(out=rstd[:, :], in0=veps[:, :], in1=expo[:, :],
                                            op=ALU.pow).then_inc(rstd_ready, 1)
                    pool.wait_ge(hn_ready, t + 1)
                    x_t = X2[:, bass.ds(t, 1), :].rearrange("p o c -> p (o c)")
                    nc.gpsimd.tensor_tensor(out=x_t, in0=hn[:, m % 2, :], in1=x_t, op=ALU.add).then_inc(sum_ready, 1)
                tiles(pool, body)

            @block.tensor
            def _(pe):
                pe.wait_ge(const_in, NCONST * 16)
                nc.tensor.matmul(QP[0:RD, 0:NS], wrT[:, :], keysT[:, :], start=True, stop=True).then_inc(rk_done, 1)
                for m in range(2):
                    for c in range(CC):
                        last = nc.tensor.matmul(AP_[:, m * BOT:(m + 1) * BOT], avT[:, c, m * P:(m + 1) * P],
                                                wvdT[:, c, :], start=c == 0, stop=c == CC - 1)
                last.then_inc(av_done, 1)

                def rows_t(t, m):
                    pe.wait_ge(hn_ready, t + 1)
                    wait(pe, ht_ready, t - 1)
                    for c in range(CC):
                        last = nc.tensor.transpose(T[:, m % 2, c, :], hn[:, m % 2, c * P:(c + 1) * P], ident[:, :])
                    last.then_inc(xt_ready, 1)

                def project(t, m):
                    pe.wait_ge(ht_ready, t + 1)
                    wait(pe, q_ready, t - 1)
                    wait(pe, cube_ready, t - 1)
                    for c in range(CC):
                        last = nc.tensor.matmul(U[:, m % 2, 0:N1], hT[:, m % 2, c, :], w1[:, c, :], start=c == 0,
                                                stop=c == CC - 1)
                    last.then_inc(um_ready, 1)

                def query_t(t, m):
                    pe.wait_ge(q_ready, t + 1)
                    wait(pe, qt_ready, t)
                    if isinstance(t, int) and t == 0:
                        pe.wait_ge(rk_ready, 1)
                    apart(pe, passed["pe"])
                    nc.tensor.transpose(QP[0:BOT, 0:P], qsb[:, m % 2, :], ident[:, :]).then_inc(qt_done, 1)

                def body(t, m, b):
                    rows_t(t, m)
                    if not (isinstance(t, int) and t < 2):
                        query_t(t - 2, m)
                    if not (isinstance(t, int) and t < 1):
                        project(t - 1, m + 1)
                tiles(pe, body)
                query_t(last_t - 1, 0)
                project(last_t, 1)
                query_t(last_t, 1)

            @block.scalar
            def _(act):
                act.wait_ge(rk_done, 1)
                nc.scalar.activation(rkT[:, :], QP[0:RD, 0:NS], ACT.Copy).then_inc(rk_ready, 1)
                act.wait_ge(av_done, 1)
                nc.scalar.activation(AV[:, :, :].rearrange("p a b -> p (a b)"), AP_[:, 0:2 * BOT],
                                     ACT.Copy).then_inc(av_ready, 1)

                def copy_t(t, m):
                    act.wait_ge(xt_ready, t + 1)
                    wait(act, um_ready, t - 1)
                    nc.scalar.activation(hT[:, m % 2, :, :], T[:, m % 2, :, :], ACT.Copy).then_inc(ht_ready, 1)

                def query(t, m):
                    act.wait_ge(um_ready, t + 1)
                    wait(act, qt_done, t - 1)
                    nc.scalar.activation(qsb[:, m % 2, :], U[:, m % 2, 0:BOT], ACT.Copy).then_inc(q_ready, 1)

                def tanh(t):
                    act.wait_ge(cube_ready, t + 1)
                    nc.scalar.activation(th[:, :], y3[:, :], ACT.Tanh,
                                         scale=0.7978845608028654).then_inc(tanh_ready, 1)

                def query_out(t):
                    act.wait_ge(qt_done, t + 1)
                    nc.scalar.activation(QT_[:, bass.ds(t * P, P)], QP[0:BOT, 0:P], ACT.Copy).then_inc(qt_ready, 1)

                def body(t, m, b):
                    copy_t(t, m)
                    if not (isinstance(t, int) and t < 2):
                        query_out(t - 2)
                    if not (isinstance(t, int) and t < 1):
                        query(t - 1, m + 1)
                        tanh(t - 1)
                tiles(act, body)
                query_out(last_t - 1)
                query(last_t, 1)
                tanh(last_t)
                query_out(last_t)

            @block.vector
            def _(dve):
                chain = Chain(dve, chain_s)
                dve.wait_ge(const_in, NCONST * 16)

                def front(t, m, b):
                    x_t = X2[:, bass.ds(t, 1), :].rearrange("p o c -> p (o c)")
                    dve.wait_ge(in_q[m], (b + 1) * 16)
                    nc.vector.bn_stats(stats[:, 0, :], X2[:, bass.ds(t, 1), 0:512].rearrange("p o c -> p (o c)"))
                    chain(nc.vector.bn_stats(stats[:, 1, :],
                                             X2[:, bass.ds(t, 1), 512:1024].rearrange("p o c -> p (o c)")))
                    apart(dve, passed["dve"])
                    chain(nc.vector.bn_aggr(mv[:, :], stats[:, :, :]))
                    nc.vector.tensor_scalar(out=veps[:, :], in0=mv[:, 1:2], scalar1=EPS, scalar2=None,
                                            op0=ALU.add).then_inc(var_ready, 1)
                    dve.wait_ge(rstd_ready, t + 1)
                    chain(nc.vector.tensor_scalar(out=varh[:, bass.ds(t, 1)], in0=mv[:, 1:2], scalar1=rstd[:, :],
                                                  scalar2=rstd[:, :], op0=ALU.mult, op1=ALU.mult))
                    wait(dve, xt_ready, t - 1)
                    wait(dve, sum_ready, t - 1)
                    nc.vector.tensor_scalar(out=hn[:, m % 2, :], in0=x_t, scalar1=mv[:, 0:1], scalar2=rstd[:, :],
                                            op0=ALU.subtract, op1=ALU.mult).then_inc(hn_ready, 1)

                def cube(t, m):
                    dve.wait_ge(q_ready, t + 1)
                    chain(nc.vector.tensor_tensor(out=y[:, :], in0=U[:, m % 2, BOT:N1], in1=bu1, op=ALU.add))
                    chain(nc.vector.tensor_tensor(out=y2[:, :], in0=y[:, :], in1=y[:, :], op=ALU.mult))
                    chain(nc.vector.tensor_scalar(out=y2[:, :], in0=y2[:, :], scalar1=0.044715, scalar2=1.0,
                                                  op0=ALU.mult, op1=ALU.add))
                    nc.vector.tensor_tensor(out=y3[:, :], in0=y2[:, :], in1=y[:, :],
                                            op=ALU.mult).then_inc(cube_ready, 1)

                def learned(t):
                    dve.wait_ge(tanh_ready, t + 1)
                    chain(nc.vector.scalar_tensor_tensor(out=y2[:, :], in0=th[:, :], scalar=1.0, in1=y[:, :],
                                                         op0=ALU.add, op1=ALU.mult))
                    apart(dve, passed["dve"])
                    chain(nc.vector.tensor_tensor_reduce(out=y[:, :], in0=y2[:, :], in1=wu2, scale=0.5, scalar=0.0,
                                                         op0=ALU.mult, op1=ALU.add, accum_out=lrn[:, :]))
                    nc.vector.tensor_copy(learn[:, bass.ds(t, 1)], lrn[:, :]).then_inc(learn_ready, 1)

                def body(t, m, b):
                    back = not (isinstance(t, int) and t < 1)
                    chain.base, chain.n = (t * (FRONT + BACK) - BACK if back else 0), 0
                    front(t, m, b)
                    if back:
                        cube(t - 1, m + 1)
                        learned(t - 1)
                    assert chain.n == FRONT + (BACK if back else 0)
                tiles(dve, body)
                chain.base, chain.n = NT * (FRONT + BACK) - BACK, 0
                cube(last_t, 1)
                learned(last_t)

        stage_e2(nc, keep, passed, ident, X2, keysT, wrT, rkT, AV, wvuT, log_rel, scal, QT_, varh, learn, out)


def stage_e2(nc, keep, passed, ident, X2, keysT, wrT, rkT, AV, wvuT, log_rel, scal, QT_, varh, learn, out):
    (ones_ready, log_ready, tot_done, chain_s, sig_in, sig_out, gate_in, gate_out, gate_ready, q_ready, rq_done,
     rq_ready, ra_done, pick_ready, chain1_s, chain2_s, w_ready, wt_done, wt_ready, tv_done, tv_ready, o_done, o_ready,
     out0, out1) = semaphores(
        nc, keep, "f", "ones_ready log_ready tot_done chain sig_in sig_out gate_in gate_out gate_ready q_ready "
        "rq_done rq_ready ra_done pick_ready chain1 chain2 w_ready wt_done wt_ready tv_done tv_ready o_done o_ready "
        "out0 out1")
    out_q = [out0, out1]
    PICK, FIN = 7, 2
    last_t = NT - 1
    k = Kit(nc, "f")
    with k.ctx:
        ones = k.sb("ones", [P, P])
        logv = k.sb("logv", [P, NT])
        lsum = k.sb("lsum", [P, 1])
        mean = k.sb("mean", [P, 1])
        half_l = k.sb("half_l", [P, NT])
        sig = k.sb("sig", [P, NT])
        u = k.sb("u", [P, NT])
        gate = k.sb("gate", [P, NT])
        big = k.sb("big", [P, NT])
        q_s = k.sb("q_s", [BOT, 2, P])
        rq = k.sb("rq", [RD, P])
        rs = k.sb("rs", [P, NS])
        top = k.sb("top", [P, 8])
        rep = k.sb("rep", [P, NS])
        at = k.sb("at", [P, NS])
        att = k.sb("att", [P, 2, NS])
        amax = k.sb("amax", [P, 1])
        nmax = k.sb("nmax", [P, 2])
        w = k.sb("w", [P, 2, NS])
        wsum = k.sb("wsum", [P, 2])
        wt = k.sb("wt", [P, 2, P])
        tv = k.sb("tv", [BOT, P])
        rws = k.sb("rws", [P, 1])
        fac = k.sb("fac", [P, 1])
        ob = k.sb("ob", [P, 2, C])
        TOT = k.ps("TOT", [P, 512])
        RQ = k.ps("RQ", [P, 512])
        RA = k.ps("RA", [P, 2, NS])
        WT = k.ps("WT", [P, 512])
        TV = k.ps("TV", [P, 512])
        OUT = k.ps("OUT", [P, 2, 512])
        block = k.ctx.enter_context(nc.Block())

        @block.sync
        def _(sp):
            def body(t, s):
                sp.wait_ge(o_ready, 2 * t + 2)
                sp.dma_start(out[bass.ds(t * P, P), :], ob[:, s, :]).then_inc(out_q[s], 16)
            pairs(sp, body, last_t)
            for s in range(2):
                sp.wait_ge(out_q[s], NT // 2 * 16)

        @block.tensor
        def _(pe):
            pe.wait_ge(ones_ready, 1)
            pe.wait_ge(log_ready, 1)
            nc.tensor.matmul(TOT[:, 0:1], ones[:, :], lsum[:, :], start=True, stop=True).then_inc(tot_done, 1)

            def route(t, s):
                pe.wait_ge(q_ready, t + 1)
                wait(pe, rq_ready, t)
                apart(pe, passed["pe"])
                nc.tensor.matmul(RQ[0:RD, 0:P], wrT[:, :], q_s[:, s, :], start=True, stop=True).then_inc(rq_done, 1)
                pe.wait_ge(rq_ready, t + 1)
                wait(pe, pick_ready, t)
                nc.tensor.matmul(RA[:, 0, :], rq[:, :], rkT[:, :], start=True, stop=True)
                nc.tensor.matmul(RA[:, 1, :], q_s[:, s, :], keysT[:, :], start=True, stop=True).then_inc(ra_done, 1)

            def retrieve(t, s):
                pe.wait_ge(w_ready, t + 1)
                wait(pe, wt_ready, t)
                for m in range(2):
                    last = nc.tensor.transpose(WT[:, m * P:(m + 1) * P], w[:, s, m * P:(m + 1) * P], ident[:, :])
                last.then_inc(wt_done, 1)
                pe.wait_ge(wt_ready, t + 1)
                wait(pe, tv_ready, t)
                for m in range(2):
                    last = nc.tensor.matmul(TV[0:BOT, 0:P], AV[:, m, :], wt[:, m, :], start=m == 0, stop=m == 1)
                last.then_inc(tv_done, 1)
                pe.wait_ge(tv_ready, t + 1)
                for m in range(2):
                    wait(pe, o_ready, 2 * t + m - 1)
                    nc.tensor.matmul(OUT[:, m, :], tv[:, :], wvuT[:, m * 512:(m + 1) * 512], start=True,
                                     stop=True).then_inc(o_done, 1)

            def body(t, s):
                route(t, s)
                if not (isinstance(t, int) and t < 1):
                    retrieve(t - 1, 1 - s)
            pairs(pe, body, last_t)
            retrieve(last_t, last_t % 2)

        @block.scalar
        def _(act):
            nc.scalar.activation(logv[:, :], varh[:, :], ACT.Ln, bias=1.0, accum_out=lsum[:, :]).then_inc(log_ready, 1)
            act.wait_ge(sig_in, 1)
            nc.scalar.activation(sig[:, :], half_l[:, :], ACT.Tanh).then_inc(sig_out, 1)
            act.wait_ge(gate_in, 1)
            nc.scalar.activation(gate[:, :], u[:, :], ACT.Tanh).then_inc(gate_out, 1)

            def query(t, s):
                wait(act, ra_done, t - 1)
                nc.scalar.activation(q_s[:, s, :], QT_[:, bass.ds(t * P, P)], ACT.Copy).then_inc(q_ready, 1)

            def routed(t):
                act.wait_ge(rq_done, t + 1)
                wait(act, ra_done, t)
                nc.scalar.activation(rq[:, :], RQ[0:RD, 0:P], ACT.Copy).then_inc(rq_ready, 1)

            def weights(t, s):
                act.wait_ge(pick_ready, t + 1)
                wait(act, wt_done, t - 1)
                wait(act, o_ready, 2 * (t - 1))
                nc.scalar.activation(w[:, s, :], att[:, s, :], ACT.Exp, bias=nmax[:, s:s + 1],
                                     accum_out=wsum[:, s:s + 1]).then_inc(w_ready, 1)

            def retrieved(t):
                act.wait_ge(wt_done, t + 1)
                wait(act, tv_done, t)
                nc.scalar.activation(wt[:, :, :].rearrange("p a b -> p (a b)"), WT[:, 0:2 * P],
                                     ACT.Copy).then_inc(wt_ready, 1)
                act.wait_ge(tv_done, t + 1)
                wait(act, o_done, 2 * t)
                nc.scalar.activation(tv[:, :], TV[0:BOT, 0:P], ACT.Copy).then_inc(tv_ready, 1)

            def body(t, s):
                query(t, s)
                routed(t)
                if not (isinstance(t, int) and t < 1):
                    retrieved(t - 1)
                weights(t, s)
            pairs(act, body, last_t)
            retrieved(last_t)

        @block.vector
        def _(dve):
            chain = Chain(dve, chain_s)
            nc.vector.memset(ones[:, :], 1.0).then_inc(ones_ready, 1)
            nc.vector.tensor_scalar(out=half_l[:, :], in0=learn[:, :], scalar1=scal[:, 0:1], scalar2=0.5,
                                    op0=ALU.add, op1=ALU.mult).then_inc(sig_in, 1)
            dve.wait_ge(tot_done, 1)
            chain(nc.vector.tensor_scalar(out=mean[:, :], in0=TOT[:, 0:1], scalar1=1.0 / TOK, scalar2=1e-6,
                                          op0=ALU.mult, op1=ALU.add))
            chain(nc.vector.reciprocal(mean[:, :], mean[:, :]))
            chain(nc.vector.tensor_scalar(out=u[:, :], in0=logv[:, :], scalar1=mean[:, :], scalar2=0.5,
                                          op0=ALU.mult, op1=ALU.mult))
            dve.wait_ge(sig_out, 1)
            chain(nc.vector.tensor_scalar(out=sig[:, :], in0=sig[:, :], scalar1=1.25, scalar2=1.25,
                                          op0=ALU.mult, op1=ALU.add))
            chain(nc.vector.tensor_tensor(out=u[:, :], in0=u[:, :], in1=sig[:, :], op=ALU.add))
            chain(nc.vector.tensor_scalar(out=u[:, :], in0=u[:, :], scalar1=0.0, scalar2=5.0,
                                          op0=ALU.max, op1=ALU.min))
            chain(nc.vector.tensor_scalar(out=u[:, :], in0=u[:, :], scalar1=0.5, scalar2=1.0 / 1.5,
                                          op0=ALU.subtract, op1=ALU.mult))
            chain(nc.vector.tensor_scalar(out=u[:, :], in0=u[:, :], scalar1=0.0, scalar2=1.0,
                                          op0=ALU.max, op1=ALU.min))
            chain(nc.vector.tensor_scalar(out=u[:, :], in0=u[:, :], scalar1=scal[:, 1:2], scalar2=scal[:, 2:3],
                                          op0=ALU.mult, op1=ALU.add))
            nc.vector.tensor_scalar(out=u[:, :], in0=u[:, :], scalar1=0.5, scalar2=None,
                                    op0=ALU.mult).then_inc(gate_in, 1)
            dve.wait_ge(gate_out, 1)
            chain(nc.vector.tensor_scalar(out=gate[:, :], in0=gate[:, :], scalar1=0.5, scalar2=0.5,
                                          op0=ALU.mult, op1=ALU.add))
            chain(nc.vector.tensor_scalar(out=big[:, :], in0=gate[:, :], scalar1=0.05, scalar2=None, op0=ALU.is_ge))
            nc.vector.tensor_tensor(out=gate[:, :], in0=gate[:, :], in1=big[:, :], op=ALU.mult).then_inc(gate_ready, 1)
            dve.wait_ge(gate_ready, 1)
            chain1, chain2 = Chain(dve, chain1_s), Chain(dve, chain2_s)

            def pick(t, s):
                chain1.base, chain1.n = t * PICK, 0
                dve.wait_ge(ra_done, t + 1)
                chain1(nc.vector.scalar_tensor_tensor(out=rs[:, :], in0=RA[:, 0, :], scalar=RD ** -0.5, in1=log_rel,
                                                      op0=ALU.mult, op1=ALU.add))
                apart(dve, passed["dve"])
                chain1(nc.vector.max(top[:, :], rs[:, :]))
                apart(dve, passed["dve"])
                chain1(nc.vector.match_replace(rep[:, :], top[:, :], rs[:, :], -3e38))
                chain1(nc.vector.tensor_tensor(out=rep[:, :], in0=rep[:, :], in1=rs[:, :], op=ALU.not_equal))
                chain1(nc.vector.tensor_scalar(out=rep[:, :], in0=rep[:, :], scalar1=1.0, scalar2=BIG,
                                               op0=ALU.subtract, op1=ALU.mult))
                chain1(nc.vector.scalar_tensor_tensor(out=at[:, :], in0=RA[:, 1, :], scalar=BOT ** -0.5, in1=log_rel,
                                                      op0=ALU.mult, op1=ALU.add))
                wait(dve, w_ready, t - 1)
                apart(dve, passed["dve"])
                chain1(nc.vector.tensor_tensor_reduce(out=att[:, s, :], in0=at[:, :], in1=rep[:, :], scale=1.0,
                                                      scalar=-3e38, op0=ALU.add, op1=ALU.max, accum_out=amax[:, :]))
                nc.vector.tensor_scalar(out=nmax[:, s:s + 1], in0=amax[:, :], scalar1=-1.0, scalar2=None,
                                        op0=ALU.mult).then_inc(pick_ready, 1)
                dve.wait_ge(pick_ready, t + 1)

            def finish(t, s):
                chain2.base, chain2.n = t * FIN, 0
                dve.wait_ge(w_ready, t + 1)
                chain2(nc.vector.reciprocal(rws[:, :], wsum[:, s:s + 1]))
                chain2(nc.vector.tensor_tensor(out=fac[:, :], in0=rws[:, :], in1=gate[:, bass.ds(t, 1)], op=ALU.mult))
                wait(dve, out_q[s], (t // 2 if isinstance(t, int) else (t - s) // 2) * 16)
                for m in range(2):
                    dve.wait_ge(o_done, 2 * t + m + 1)
                    nc.vector.scalar_tensor_tensor(
                        out=ob[:, s, m * 512:(m + 1) * 512], in0=OUT[:, m, :], scalar=fac[:, :],
                        in1=X2[:, bass.ds(t, 1), m * 512:(m + 1) * 512].rearrange("p o c -> p (o c)"),
                        op0=ALU.mult, op1=ALU.add).then_inc(o_ready, 1)
                dve.wait_ge(o_ready, 2 * t + 2)

            def body(t, s):
                pick(t, s)
                if not (isinstance(t, int) and t < 1):
                    finish(t - 1, 1 - s)
            pairs(dve, body, last_t)
            finish(last_t, last_t % 2)


def program(nc, a, out):
    qk_hi = nc.dram_tensor("qk_hi", [2 * B * C, S], F32, kind="Internal").ap()
    qk_lo = nc.dram_tensor("qk_lo", [2 * B * C, S], F32, kind="Internal").ap()
    v_dram = nc.dram_tensor("v_dram", [ITS * S, P], F32, kind="Internal").ap()
    ao_hi = nc.dram_tensor("ao_hi", [B * C, S], F32, kind="Internal").ap()
    ao_lo = nc.dram_tensor("ao_lo", [B * C, S], F32, kind="Internal").ap()
    x1 = nc.dram_tensor("x1", [ITS * S, P], F32, kind="Internal").ap()
    x2 = nc.dram_tensor("x2", [ITS * S, P], F32, kind="Internal").ap()
    q2_hi = nc.dram_tensor("q2_hi", [B * C, S], F32, kind="Internal").ap()
    q2_lo = nc.dram_tensor("q2_lo", [B * C, S], F32, kind="Internal").ap()
    with ExitStack() as keep:
        passed = dict(zip(("pe", "dve", "pool", "sp"), semaphores(nc, keep, "passed", "pe dve pool sp")))
        stage_a(nc, keep, passed, a["x"], a["wqkvT"], a["rope"], a["ident"], qk_hi, qk_lo, v_dram)
        cross, proj = Kit(nc, "cross"), Kit(nc, "proj")
        mask_in, wo_in = semaphores(nc, keep, "early", "mask_in wo_in")
        with cross.ctx:
            mask = cross.sb("mask", [P, QT, KP])
            with proj.ctx:
                wo = proj.sb("wo", [P, CC, C])
                early = ((wo[:, :, :], a["woT"].rearrange("(c p) n -> p c n", p=P), wo_in),
                         (mask[:, :, :], a["mask"], mask_in))
                stage_b(nc, keep, passed, early, a["ident"], a["causal"], qk_hi, qk_lo, v_dram, ao_hi, ao_lo)
                stage_c(nc, keep, passed, wo, wo_in, mask, mask_in, a["x"], a["ident"], ao_hi, ao_lo, x1,
                        q2_hi, q2_lo)
            stage_d(nc, keep, passed, mask, a["ident"], a["ctxT"], a["ctxV"], a["low_rows"], q2_hi, q2_lo, x1, x2)
        stage_e(nc, keep, passed, a["ident"], a["w1"], a["wrT"], a["keysT"], a["avT"], a["wvdT"], a["wvuT"], a["vecs"],
                a["scal"], x2, out)


def constants():
    import numpy as np
    f = np.float32
    theta = (f(1.0) / f(10000.0) ** (np.arange(0, D, 2, dtype=f) / f(D))).astype(f)
    angle = np.outer(np.arange(S, dtype=f), theta).astype(f)
    angle = np.concatenate([angle, angle], -1)
    cos, sin = np.cos(angle).astype(f), np.sin(angle).astype(f)
    sin[:, :D // 2] *= -1
    scale = f(-1.0 / np.sqrt(D))
    tab = np.stack([np.stack([cos * scale, sin * scale]), np.stack([cos, sin])]).astype(f)
    rope = np.ascontiguousarray(tab.reshape(2, 2, QT, P, D).transpose(3, 0, 1, 2, 4))
    causal = np.zeros((P, S), f)
    causal[:, S - P:] = np.where(np.arange(P)[None, :] > np.arange(P)[:, None], f(BIG), f(0))
    return {"ident": np.eye(P, dtype=f), "rope": rope, "causal": causal,
            "low_rows": np.repeat(np.array([0, -1, 0, -1], f), D).reshape(P, 1)}


def layout(i):
    import numpy as np
    g = {n: np.asarray(v) for n, v in i.items()}

    def chunks(w):
        return np.ascontiguousarray(w.reshape(CC, P, -1).transpose(1, 0, 2))

    ctx = g["ctx_1024"]
    keys = np.zeros((B, KC * P, G, D), ctx.dtype)
    keys[:, :KEYS] = ctx.reshape(B, KEYS, G, D)
    mask = np.full((S, KP), -BIG, np.float32)
    mask[:, :KEYS] = g["mask_SxS2_ff0"]
    return {
        "x": g["x"].reshape(TOK, C),
        "woT": np.ascontiguousarray(g["L0_attn_wo"].T),
        "ctxT": np.ascontiguousarray(keys[:, :KP].transpose(0, 2, 3, 1)).reshape(ITS * D, KP),
        "ctxV": np.ascontiguousarray(keys.reshape(B, KC, P, G, D).transpose(0, 3, 2, 1, 4)).reshape(ITS * P, KC, D),
        "mask": np.ascontiguousarray(mask.reshape(QT, P, KP).transpose(1, 0, 2)),
        "wqkvT": np.ascontiguousarray(np.concatenate([g["L0_attn_wq"], g["L0_attn_wk"], g["L0_attn_wv"]]).T),
        "w1": chunks(np.concatenate([g["L0_ffn_Wq"], g["L0_ffn_Wu1"]]).T),
        "wrT": np.ascontiguousarray(g["L0_ffn_Wr"].T),
        "keysT": np.ascontiguousarray(g["L0_ffn_aux_keys"].T),
        "avT": chunks(g["L0_ffn_aux_values"].T),
        "wvdT": chunks(g["L0_ffn_Wvd"].T),
        "wvuT": np.ascontiguousarray(g["L0_ffn_Wvu"].T),
        "vecs": np.concatenate([g["L0_ffn_log_rel"], g["L0_ffn_bu1"], g["L0_ffn_Wu2"][0]]),
        "scal": np.concatenate([g["L0_ffn_bu2"], g["L0_ffn_gate_w1"].reshape(1), g["L0_ffn_gate_bias"].reshape(1)]),
        **constants(),
    }


def kernel(**inputs):
    import numpy as np
    import concourse.bacc as bacc
    from concourse.bass_utils import run_bass_kernel_spmd

    nc = bacc.Bacc("TRN2", target_bir_lowering=False, num_devices=1)
    arrays = layout(inputs)
    aps = {n: nc.dram_tensor(f"in_{n}", v.shape, mybir.dt.from_np(v.dtype), kind="ExternalInput").ap()
           for n, v in arrays.items()}
    out = nc.dram_tensor("out_x", [TOK, C], F32, kind="ExternalOutput").ap()
    program(nc, aps, out)
    r = run_bass_kernel_spmd(nc, [{f"in_{n}": v for n, v in arrays.items()}], core_ids=[0])
    return np.asarray(r.results[0]["out_x"]).reshape(B, S, C)
```

```python
from contextlib import ExitStack

import concourse.bass as bass
from concourse import mybir
from concourse.alu_op_type import AluOpType as ALU

F32 = mybir.dt.float32
F32R = mybir.dt.float32r
ACT = mybir.ActivationFunctionType
AX = mybir.AxisListType

P = 128
B, S, C = 4, 512, 1024
H, D = 32, 32
G = 8
R = H // G
TOK = B * S
NT = TOK // P
QT = S // P
CC = C // P
KEYS = 1601
KP = 1608
KC = (KP + P - 1) // P
KLAST = KP - (KC - 1) * P
KQ = KP // 4
EPS = 1e-5
BIG = 1e38
ITS = B * G
NS, BOT, RD, HU = 256, 64, 48, 256


class Chain:

    def __init__(self, eng, sem):
        self.eng, self.sem, self.base, self.n = eng, sem, 0, 0

    def mark(self, ins):
        ins.then_inc(self.sem, 1)
        self.n += 1

    def settle(self):
        self.eng.wait_ge(self.sem, self.base + self.n)

    def __call__(self, ins):
        self.mark(ins)
        self.settle()


class Kit:

    def __init__(self, nc, name):
        self.nc, self.name, self.ctx = nc, name, ExitStack()

    def sb(self, name, shape, dt=F32):
        return self.ctx.enter_context(self.nc.sbuf_tensor(f"{self.name}_{name}", shape, dt))

    def ps(self, name, shape, dt=F32):
        return self.ctx.enter_context(self.nc.psum_tensor(f"{self.name}_{name}", shape, dt))


def semaphores(nc, keep, stage, names):
    return [keep.enter_context(nc.semaphore(f"{stage}_{n}")) for n in names.split()]


def stage_a(nc, keep, passed, x, wqkvT, rope, ident_d, qk_hi, qk_lo, v_dram):
    HT = NT // 2
    HTOK = HT * P
    NJ = 6
    NR = 4
    PARTS = 4
    PC = CC // PARTS
    STEPS = 2 * NJ
    SLOTS = [(J, t) for J in range(STEPS) for t in range(HT)]
    k = Kit(nc, "a")
    (x_in0, x_in1, var_ready, rstd_ready, xn_ready, xt_ready, xhi_ready, xlo_ready, chain_s, const_in,
     w_in0, w_in1, w_in2, w_in3, whi_ready, wlo_ready, mm_done, ab_ready, roped, rt_ready, shi_ready, slo_ready,
     st_out0, st_out1, v_ready, v_out0, v_out1, expo_ready) = semaphores(
        nc, keep, "a", "x_in0 x_in1 var_ready rstd_ready xn_ready xt_ready xhi_ready xlo_ready chain const_in "
        "w_in0 w_in1 w_in2 w_in3 whi_ready wlo_ready mm_done ab_ready roped rt_ready shi_ready slo_ready "
        "st_out0 st_out1 v_ready v_out0 v_out1 expo_ready")
    x_in, st_out, v_out, w_in = [x_in0, x_in1], [st_out0, st_out1], [v_out0, v_out1], [w_in0, w_in1, w_in2, w_in3]

    def tiles_before(J, t, roped_):
        return sum((j % NJ < NR) == roped_ for j, m in SLOTS[:J * HT + t])

    def rope_tile(J, t):
        return tiles_before(J, t, True) if J % NJ < NR else None

    def behind(J, t):
        if J * HT + t == 0:
            return None
        j, m = SLOTS[J * HT + t - 1]
        r = rope_tile(j, m)
        return None if r is None else (j, m, r)

    def norm_in(J, t):
        if J == 0 and t + 2 < HT:
            return t + 2
        if J == NJ - 1:
            return HT + t
        return None

    with k.ctx:
        ident = k.sb("ident", [P, P])
        rope_sb = k.sb("rope", [P, 2, 2, QT, D])
        xb = k.sb("x", [P, 2, C])
        xn = k.sb("xn", [P, 2, C])
        stats = k.sb("stats", [P, 2, 6])
        mv = k.sb("mv", [P, 2, 2])
        veps = k.sb("veps", [P, 2])
        rstd = k.sb("rstd", [P, 2])
        expo = k.sb("expo", [P, 1])
        XH = k.sb("XH", [P, CC, HTOK], F32R)
        XL = k.sb("XL", [P, CC, HTOK], F32R)
        wraw = k.sb("wraw", [P, CC, 512])
        WH = k.sb("WH", [P, 2, CC, 512], F32R)
        WL = k.sb("WL", [P, 2, CC, 512], F32R)
        qcos = k.sb("qcos", [P, 2, 512])
        qsin = k.sb("qsin", [P, 2, 512])
        qr = k.sb("qr", [P, 2, 512])
        st_hi = k.sb("st_hi", [P, 2, 4, P], F32R)
        st_lo = k.sb("st_lo", [P, 2, 4, P], F32R)
        vst = k.sb("vst", [P, 2, 512])
        Tx = k.ps("Tx", [P, CC, P])
        T = k.ps("T", [P, 2, 4, P])
        M = k.ps("M", [P, 4, 512])
        block = k.ctx.enter_context(nc.Block())

        @block.sync
        def _(sp):
            def load_x(u):
                wait(sp, xn_ready, u - 1)
                sp.dma_start(xb[:, u % 2, :], x[u * P:(u + 1) * P, :]).then_inc(x_in[u % 2], 16)

            def load_w(J):
                for p in range(PARTS):
                    wait(sp, whi_ready, (J - 1) * PARTS + p + 1)
                    wait(sp, wlo_ready, (J - 1) * PARTS + p + 1)
                    rows = slice(p * PC * P, (p + 1) * PC * P)
                    sp.dma_start(wraw[:, p * PC:(p + 1) * PC, :],
                                 wqkvT[rows, (J % NJ) * 512:(J % NJ + 1) * 512]
                                 .rearrange("(c p) n -> p c n", p=P)).then_inc(w_in[p], 16)

            def store(J, t):
                h, j = J // NJ, J % NJ
                b = h * 2 + t // QT
                if j < NR:
                    kq, cols, r = j // 2, (j % 2) * 512, rope_tile(J, t)
                    row = (kq * B + b) * C + cols
                    for ready, buf, dst in ((shi_ready, st_hi, qk_hi), (slo_ready, st_lo, qk_lo)):
                        sp.wait_ge(ready, r + 1)
                        sp.dma_start(dst[row:row + 512, (t % QT) * P:(t % QT + 1) * P]
                                     .rearrange("(c p) t -> p c t", p=P),
                                     buf[:, r % 2, :, :].bitcast(F32)).then_inc(st_out[r % 2], 16)
                else:
                    n = tiles_before(J, t, False)
                    sp.wait_ge(v_ready, n + 1)
                    row = (b * G + (j - NR) * 4) * S
                    sp.dma_start(v_dram[row:row + 4 * S, :].rearrange("(g q p) c -> q p g c", q=QT, p=P)[t % QT],
                                 vst[:, n % 2, :].rearrange("p (g c) -> p g c", g=4)).then_inc(v_out[n % 2], 16)

            load_x(0)
            sp.dma_start(ident[:, :], ident_d).then_inc(const_in, 16)
            load_x(1)
            sp.dma_start(rope_sb[:, :, :, :, :], rope).then_inc(const_in, 16)
            load_w(0)
            for n, (J, t) in enumerate(SLOTS):
                u = norm_in(J, t)
                if u is not None and u < HT:
                    load_x(u)
                if J == NJ - 1 and t == 0:
                    load_x(HT)
                if J == NJ - 1 and t + 1 < HT:
                    load_x(HT + t + 1)
                if n == 0:
                    load_w(1)
                if t == 5 and J + 2 < STEPS:
                    load_w(J + 2)
                if n >= 2:
                    store(*SLOTS[n - 2])
            store(*SLOTS[-2])
            store(*SLOTS[-1])
            for s in range(2):
                sp.wait_ge(st_out[s], 2 * NR * HT * 16)
                sp.wait_ge(v_out[s], (NJ - NR) * HT * 16)

        @block.gpsimd
        def _(pool):
            def power(u):
                pool.wait_ge(var_ready, u + 1)
                nc.gpsimd.tensor_tensor(out=rstd[:, u % 2:u % 2 + 1], in0=veps[:, u % 2:u % 2 + 1],
                                        in1=expo[:, :], op=ALU.pow).then_inc(rstd_ready, 1)

            pool.memset(expo[:, :], -0.5).then_inc(expo_ready, 1)
            pool.wait_ge(expo_ready, 1)
            power(0)
            power(1)
            for J, t in SLOTS:
                u = norm_in(J, t)
                if u is not None:
                    power(u)
                r = rope_tile(J, t)
                if r is not None:
                    pool.wait_ge(ab_ready, r + 1)
                    wait(pool, rt_ready, r - 1)
                    nc.gpsimd.tensor_tensor(out=qr[:, r % 2, :], in0=qcos[:, r % 2, :],
                                            in1=qsin[:, r % 2, :], op=ALU.add).then_inc(roped, 1)

        @block.scalar
        def _(act):
            def split_w(J, parts=range(PARTS)):
                for p in parts:
                    act.wait_ge(w_in[p], (J + 1) * 16)
                    wait(act, mm_done, (J - 1) * HT)
                    nc.scalar.activation(WH[:, J % 2, p * PC:(p + 1) * PC, :], wraw[:, p * PC:(p + 1) * PC, :],
                                         ACT.Copy).then_inc(whi_ready, 1)

            def xhi(u):
                act.wait_ge(xt_ready, u + 1)
                if u >= HT:
                    act.wait_ge(mm_done, (NJ - 1) * HT + u - HT + 1)
                nc.scalar.activation(XH[:, :, (u % HT) * P:(u % HT + 1) * P], Tx[:, :, :],
                                     ACT.Copy).then_inc(xhi_ready, 1)

            def shi(r):
                act.wait_ge(rt_ready, r + 1)
                wait(act, st_out[r % 2], r // 2 * 32)
                nc.scalar.activation(st_hi[:, r % 2, :, :], T[:, r % 2, :, :], ACT.Copy).then_inc(shi_ready, 1)

            xhi(0)
            split_w(0, range(2))
            xhi(1)
            split_w(0, range(2, PARTS))
            for J, t in SLOTS:
                u = norm_in(J, t)
                if u is not None:
                    xhi(u)
                before = behind(J, t)
                if before:
                    shi(before[2])
                if J == 0 and t == 2:
                    split_w(1)
                if t == HT - 1 and J + 2 < STEPS:
                    split_w(J + 2)

        @block.vector
        def _(dve):
            chain = Chain(dve, chain_s)

            def split_w(J, parts=range(PARTS)):
                for p in parts:
                    dve.wait_ge(whi_ready, J * PARTS + p + 1)
                    nc.vector.tensor_tensor(out=WL[:, J % 2, p * PC:(p + 1) * PC, :],
                                            in0=wraw[:, p * PC:(p + 1) * PC, :],
                                            in1=WH[:, J % 2, p * PC:(p + 1) * PC, :].bitcast(F32),
                                            op=ALU.subtract).then_inc(wlo_ready, 1)

            def norm(u):
                s = u % 2
                dve.wait_ge(x_in[s], (u // 2 + 1) * 16)
                nc.vector.bn_stats(stats[:, 0, :], xb[:, s, 0:512])
                chain(nc.vector.bn_stats(stats[:, 1, :], xb[:, s, 512:1024]))
                chain(nc.vector.bn_aggr(mv[:, s, :], stats[:, :, :]))
                nc.vector.tensor_scalar(out=veps[:, s:s + 1], in0=mv[:, s, 1:2], scalar1=EPS, scalar2=None,
                                        op0=ALU.add).then_inc(var_ready, 1)
                dve.wait_ge(rstd_ready, u + 1)
                wait(dve, xt_ready, u - 1)
                nc.vector.tensor_scalar(out=xn[:, s, :], in0=xb[:, s, :], scalar1=mv[:, s, 0:1],
                                        scalar2=rstd[:, s:s + 1], op0=ALU.subtract,
                                        op1=ALU.mult).then_inc(xn_ready, 1)

            def xlo(u):
                dve.wait_ge(xhi_ready, u + 1)
                cols = slice((u % HT) * P, (u % HT + 1) * P)
                nc.vector.tensor_tensor(out=XL[:, :, cols], in0=Tx[:, :, :], in1=XH[:, :, cols].bitcast(F32),
                                        op=ALU.subtract).then_inc(xlo_ready, 1)

            def rotate(J, t, r):
                s, kq = r % 2, J % NJ // 2
                wait(dve, roped, r - 1)
                heads = M[:, (J * HT + t) % 4, :].rearrange("p (h d) -> p h d", d=D)
                cos = rope_sb[:, kq, 0, t % QT, :].unsqueeze(1).broadcast_to([P, 16, D])
                sin = rope_sb[:, kq, 1, t % QT, :].unsqueeze(1).broadcast_to([P, 16, D])
                oc = qcos[:, s, :].rearrange("p (h d) -> p h d", d=D)
                os = qsin[:, s, :].rearrange("p (h d) -> p h d", d=D)
                nc.vector.tensor_tensor(out=oc, in0=heads, in1=cos, op=ALU.mult)
                for lo, hi in ((0, 16), (16, 0)):
                    last = nc.vector.tensor_tensor(out=os[:, :, lo:lo + 16], in0=heads[:, :, hi:hi + 16],
                                                   in1=sin[:, :, lo:lo + 16], op=ALU.mult)
                last.then_inc(ab_ready, 1)

            def slo(r):
                s = r % 2
                dve.wait_ge(shi_ready, r + 1)
                wait(dve, st_out[s], r // 2 * 32)
                nc.vector.tensor_tensor(out=st_lo[:, s, :, :], in0=T[:, s, :, :],
                                        in1=st_hi[:, s, :, :].bitcast(F32), op=ALU.subtract).then_inc(slo_ready, 1)

            norm(0)
            norm(1)
            xlo(0)
            split_w(0, range(2))
            xlo(1)
            split_w(0, range(2, PARTS))
            dve.wait_ge(const_in, 32)
            for n, (J, t) in enumerate(SLOTS):
                u = norm_in(J, t)
                if u is not None:
                    norm(u)
                r = rope_tile(J, t)
                dve.wait_ge(mm_done, n + 1)
                if r is not None:
                    rotate(J, t, r)
                else:
                    v = tiles_before(J, t, False)
                    wait(dve, v_out[v % 2], v // 2 * 16)
                    nc.vector.tensor_copy(vst[:, v % 2, :], M[:, n % 4, :]).then_inc(v_ready, 1)
                if u is not None:
                    xlo(u)
                before = behind(J, t)
                if before:
                    slo(before[2])
                if J == 0 and t == 2:
                    split_w(1)
                if t == HT - 1 and J + 2 < STEPS:
                    split_w(J + 2)

        @block.tensor
        def _(pe):
            def rows_t(u):
                pe.wait_ge(xn_ready, u + 1)
                wait(pe, xlo_ready, u)
                for c in range(CC):
                    last = nc.tensor.transpose(Tx[:, c, :], xn[:, u % 2, c * P:(c + 1) * P], ident[:, :])
                last.then_inc(xt_ready, 1)

            def heads_t(r):
                pe.wait_ge(roped, r + 1)
                wait(pe, slo_ready, r - 1)
                for c in range(4):
                    last = nc.tensor.transpose(T[:, r % 2, c, :], qr[:, r % 2, c * P:(c + 1) * P], ident[:, :])
                last.then_inc(rt_ready, 1)

            def project(J, t):
                n = J * HT + t
                pe.wait_ge(xhi_ready, J // NJ * HT + t + 1)
                pe.wait_ge(xlo_ready, J // NJ * HT + t + 1)
                if n >= 4:
                    j, m = SLOTS[n - 4]
                    if rope_tile(j, m) is not None:
                        pe.wait_ge(ab_ready, rope_tile(j, m) + 1)
                    else:
                        pe.wait_ge(v_ready, tiles_before(j, m, False) + 1)
                for c in range(CC):
                    if t == 0 and c % PC == 0:
                        pe.wait_ge(whi_ready, J * PARTS + c // PC + 1)
                        pe.wait_ge(wlo_ready, J * PARTS + c // PC + 1)
                    for q, (a, w) in enumerate(((XH, WH), (XL, WH), (XH, WL))):
                        last = nc.tensor.matmul(M[:, n % 4, :], a[:, c, t * P:(t + 1) * P], w[:, J % 2, c, :],
                                                start=c == 0 and q == 0, stop=c == CC - 1 and q == 2)
                last.then_inc(mm_done, 1)

            pe.wait_ge(const_in, 32)
            rows_t(0)
            rows_t(1)
            for J, t in SLOTS:
                project(J, t)
                u = norm_in(J, t)
                if u is not None:
                    rows_t(u)
                before = behind(J, t)
                if before:
                    heads_t(before[2])


def wait(eng, sem, value):
    if not isinstance(value, int) or value > 0:
        eng.wait_ge(sem, value)


def apart(eng, sem):
    eng.sem_inc(sem, 1)


def pairs(eng, body, last):
    for it in (0, 1):
        body(it, it % 2)
    with eng.Fori(1, last // 2) as i:
        for s in (0, 1):
            body(2 * i + s, s)
    for it in (last - 1, last):
        body(it, it % 2)


class Keys:

    def __init__(self, nc, keep, kit):
        self.raw = kit.sb("kraw", [P, KP])
        self.K = kit.sb("K", [P, 2, KP], F32R)
        self.lows = kit.sb("lows", [P, 1])
        self.raw_in, self.raw_hi, self.ready, self.lows_in = semaphores(nc, keep, "keys", "raw_in raw_hi ready lows_in")


def stage_b(nc, keep, passed, early, ident_d, causal_d, qk_hi, qk_lo, v_dram, ao_hi, ao_lo):
    NB = R * QT
    LAG = 4
    AHEAD = LAG + 1
    RING = 8
    NLOAD = 8
    SC_BANK = [n % 3 for n in range(NB - 1)] + [1]
    T_BANK = [n % 4 for n in range(NB)]
    VALUES_AT = {1: 0, 3: 1, 5: 2, 7: 3}
    SPREAD_AT = 11
    INVERT_AT, OUT_AT, SCALE_AT = 3, 11, 15
    SPLIT_HI_AT, SPLIT_LO_AT = 3, 5
    ON_ACT = [n for n in range(NB) if n % 2 == 0]
    k = Kit(nc, "b")
    (const_in, in0, in1, v_in0, v_in1, sc_done, mx_done, ex_done, tr_done, ev_act, ev_dve, pv_done,
     osb_ready, rinv_ready, rexp_ready, rb_ready, ao_ready, aoh_ready, aol_ready, out0, out1) = semaphores(
        nc, keep, "b", "const_in in0 in1 v_in0 v_in1 sc_done mx_done ex_done tr_done ev_act ev_dve pv_done "
        "osb_ready rinv_ready rexp_ready rb_ready ao_ready aoh_ready aol_ready out0 out1")
    in_q, v_in, out_q = [in0, in1], [v_in0, v_in1], [out0, out1]

    def evac_done(eng, count):
        it, n = count
        wait(eng, ev_act, it * len(ON_ACT) + sum(m < n for m in ON_ACT))
        wait(eng, ev_dve, it * (NB - len(ON_ACT)) + sum(m < n for m in range(NB) if m not in ON_ACT))

    with k.ctx:
        ident = k.sb("ident", [P, P])
        causal = k.sb("causal", [P, S])
        Q = k.sb("Q", [P, 2, R, S], F32R)
        K = k.sb("K", [P, 2, R, S], F32R)
        V = k.sb("V", [P, 2, QT, P])
        prob = k.sb("prob", [P, RING, S])
        PT = k.sb("PT", [P, 2, R, QT, S])
        nmax = k.sb("nmax", [P, 2, NB])
        rsum = k.sb("rsum", [P, 2, NB])
        rinv = k.sb("rinv", [P, 2, NB])
        rexp = k.sb("rexp", [P, QT, R, D])
        ao = k.sb("ao", [P, S])
        aoh = k.sb("aoh", [P, 2, S], F32R)
        aol = k.sb("aol", [P, 2, S], F32R)
        SC = k.ps("SC", [P, 3, S])
        T = k.ps("T", [P, 4, S])
        O = k.ps("O", [P, S])
        block = k.ctx.enter_context(nc.Block())
        last_it = ITS - 1

        def turn(it, s):
            return it // 2 if isinstance(it, int) else (it - s) // 2

        def before(it, n, banks):
            m = next(m for m in range(n - 1, n - NB - 1, -1) if banks[m % NB] == banks[n])
            return (it, m) if m >= 0 else (it - 1, m + NB)

        def inside(it):
            return not isinstance(it, int) or 0 <= it <= last_it

        def shifted(it, n, s, by):
            n += by
            if 0 <= n < NB:
                return it, n, s
            step = 1 if n >= NB else -1
            return (it + step, n - step * NB, 1 - s) if inside(it + step) else None

        @block.sync
        def _(sp):
            def load(it, s):
                wait(sp, sc_done, (it - 1) * NB)
                for buf, kq, order in ((Q, 0, (qk_hi, qk_hi, qk_lo, qk_lo)), (K, 1, (qk_hi, qk_lo, qk_hi, qk_lo))):
                    for r, src in enumerate(order):
                        sp.dma_start(buf[32 * r:32 * r + 32, s, :, :].bitcast(F32),
                                     src[bass.ds(kq * B * C + it * P, P), :]
                                     .rearrange("(j p) t -> p j t", p=D)).then_inc(in_q[s], 16)
                wait(sp, pv_done, it - 1)
                sp.dma_start(V[:, s, :, :], v_dram[bass.ds(it * S, S), :]
                             .rearrange("(k p) d -> p k d", p=P)).then_inc(v_in[s], 16)

            def store(it, s):
                for ready, buf, dst in ((aoh_ready, aoh, ao_hi), (aol_ready, aol, ao_lo)):
                    sp.wait_ge(ready, it + 1)
                    sp.dma_start(dst[bass.ds(it * P, P), :], buf[:, s, :].bitcast(F32)).then_inc(out_q[s], 16)

            def body(it, s):
                if not (isinstance(it, int) and it == last_it):
                    load(it + 1, 1 - s)
                if isinstance(it, int) and it in early:
                    for dst, src, signal in early[it]:
                        sp.dma_start(dst, src).then_inc(signal, 16)
                if not (isinstance(it, int) and it < 2):
                    store(it - 2, s)

            sp.dma_start(ident[:, :], ident_d).then_inc(const_in, 16)
            sp.dma_start(causal[:, :], causal_d).then_inc(const_in, 16)
            load(0, 0)
            pairs(sp, body, last_it)
            store(last_it - 1, 1 - last_it % 2)
            store(last_it, last_it % 2)
            for s in range(2):
                sp.wait_ge(out_q[s], ITS // 2 * 32)

        @block.gpsimd
        def _(pool):
            def body(it, s):
                pool.wait_ge(rinv_ready, it + 1)
                wait(pool, rb_ready, it)
                apart(pool, passed["pool"])
                nc.gpsimd.tensor_copy(rexp[:, :, :, :], rinv[:, s, :].rearrange("p (j q) -> p q j", q=QT)
                                      .unsqueeze(3).broadcast_to([P, QT, R, D])).then_inc(rexp_ready, 1)
            pairs(pool, body, last_it)

        @block.tensor
        def _(pe):
            def scores(it, n, s):
                j, qt = n // QT, n % QT
                if n == 0:
                    pe.wait_ge(in_q[s], (turn(it, s) + 1) * 16 * NLOAD)
                i, m = before(it, n, SC_BANK)
                wait(pe, mx_done, i * NB + m + 1)
                cols = max((qt + 1) * P, 256)
                nc.tensor.matmul(SC[:, SC_BANK[n], 0:cols], Q[:, s, j, qt * P:(qt + 1) * P], K[:, s, j, 0:cols],
                                 start=True, stop=True).then_inc(sc_done, 1)

            def transposes(it, n, s):
                pe.wait_ge(ex_done, it * NB + n + 1)
                i, m = before(it, n, T_BANK)
                evac_done(pe, (i, m + 1))
                for c in range(n % QT + 1):
                    last = nc.tensor.transpose(T[:, T_BANK[n], c * P:(c + 1) * P], prob[:, n % RING, c * P:(c + 1) * P],
                                               ident[:, :])
                last.then_inc(tr_done, 1)

            def values(it, c, s):
                if c == 0:
                    pe.wait_ge(v_in[s], (turn(it, s) + 1) * 16)
                    evac_done(pe, (it + 1, 0))
                    wait(pe, ao_ready, it)
                for j in range(R):
                    last = nc.tensor.matmul(O[32 * j:32 * j + 32, c * P:S], V[:, s, c, 32 * j:32 * j + 32],
                                            PT[:, s, j, c, c * P:S], start=c == 0, stop=c == QT - 1)
                if c == QT - 1:
                    last.then_inc(pv_done, 1)

            def spread(it):
                pe.wait_ge(rexp_ready, it + 1)
                pe.wait_ge(osb_ready, it + 1)
                for qt in range(QT):
                    last = nc.tensor.transpose(O[:, qt * P:(qt + 1) * P],
                                               rexp[:, qt, :, :].rearrange("p j d -> p (j d)"), ident[:, :])
                last.then_inc(rb_ready, 1)

            def behind(it, n, s):
                if n in VALUES_AT:
                    values(it - 1, VALUES_AT[n], 1 - s)
                if n == SPREAD_AT:
                    spread(it - 1)

            def body(it, s):
                for n in range(NB):
                    ahead = shifted(it, n, s, AHEAD)
                    if ahead:
                        scores(*ahead)
                    transposes(it, n, s)
                    if not (isinstance(it, int) and it == 0):
                        behind(it, n, s)

            pe.wait_ge(const_in, 32)
            for n in range(AHEAD):
                scores(0, n, 0)
            pairs(pe, body, last_it)
            for n in range(NB):
                behind(ITS, n, ITS % 2)

        @block.scalar
        def _(act):
            def exponent(it, n, s):
                act.wait_ge(mx_done, it * NB + n + 1)
                row = prob[:, n % RING, 0:(n % QT + 1) * P]
                nc.scalar.activation(row, row, ACT.Exp,
                                     bias=nmax[:, s, n:n + 1], scale=-1.0,
                                     accum_out=rsum[:, s, n:n + 1]).then_inc(ex_done, 1)

            def evac(it, n, s):
                j, qt = n // QT, n % QT
                if n == ON_ACT[0]:
                    wait(act, pv_done, it - 1)
                act.wait_ge(tr_done, it * NB + n + 1)
                nc.scalar.activation(PT[:, s, j, 0:qt + 1, qt * P:(qt + 1) * P],
                                     T[:, T_BANK[n], 0:(qt + 1) * P].rearrange("p (c t) -> p c t", t=P),
                                     ACT.Copy).then_inc(ev_act, 1)

            def copy_out(it):
                act.wait_ge(pv_done, it + 1)
                wait(act, aol_ready, it)
                nc.scalar.activation(ao[:, :], O[:, :], ACT.Copy).then_inc(osb_ready, 1)

            def split(it, s):
                act.wait_ge(ao_ready, it + 1)
                wait(act, out_q[s], turn(it, s) * 32)
                nc.scalar.activation(aoh[:, s, :], ao[:, :], ACT.Copy).then_inc(aoh_ready, 1)

            def behind(it, n, s):
                old = shifted(it, n, s, -LAG)
                if old and old[1] in ON_ACT and inside(old[0]):
                    evac(*old)
                if n == OUT_AT and inside(it - 1):
                    copy_out(it - 1)
                if n == SPLIT_HI_AT and inside(it - 2):
                    split(it - 2, s)

            def body(it, s):
                for n in range(NB):
                    exponent(it, n, s)
                    behind(it, n, s)

            pairs(act, body, last_it)
            for it in (ITS, ITS + 1):
                for n in range(NB):
                    behind(it, n, it % 2)

        @block.vector
        def _(dve):
            def maxima(it, n, s):
                qt = n % QT
                cols = (qt + 1) * P
                dve.wait_ge(sc_done, it * NB + n + 1)
                wait(dve, tr_done, it * NB + n - RING + 1)
                apart(dve, passed["dve"])
                nc.vector.tensor_tensor_reduce(out=prob[:, n % RING, 0:cols], in0=SC[:, SC_BANK[n], 0:cols],
                                               in1=causal[:, S - cols:S], scale=1.0, scalar=3e38, op0=ALU.add,
                                               op1=ALU.min, accum_out=nmax[:, s, n:n + 1]).then_inc(mx_done, 1)

            def evac(it, n, s):
                j, qt = n // QT, n % QT
                if n == 0:
                    wait(dve, pv_done, it - 1)
                dve.wait_ge(tr_done, it * NB + n + 1)
                nc.vector.tensor_copy(PT[:, s, j, 0:qt + 1, qt * P:(qt + 1) * P],
                                      T[:, T_BANK[n], 0:(qt + 1) * P].rearrange("p (c t) -> p c t", t=P)).then_inc(ev_dve, 1)

            def invert(it, s):
                dve.wait_ge(ex_done, (it + 1) * NB)
                nc.vector.reciprocal(rinv[:, s, :], rsum[:, s, :]).then_inc(rinv_ready, 1)

            def scale(it):
                dve.wait_ge(osb_ready, it + 1)
                dve.wait_ge(rb_ready, it + 1)
                nc.vector.tensor_tensor(out=ao[:, :], in0=O[:, :], in1=ao[:, :], op=ALU.mult).then_inc(ao_ready, 1)

            def split(it, s):
                dve.wait_ge(aoh_ready, it + 1)
                nc.vector.tensor_tensor(out=aol[:, s, :], in0=ao[:, :], in1=aoh[:, s, :].bitcast(F32),
                                        op=ALU.subtract).then_inc(aol_ready, 1)

            def behind(it, n, s):
                old = shifted(it, n, s, -LAG)
                if old and old[1] not in ON_ACT and inside(old[0]):
                    evac(*old)
                if n == INVERT_AT and inside(it - 1):
                    invert(it - 1, 1 - s)
                if n == SCALE_AT and inside(it - 1):
                    scale(it - 1)
                if n == SPLIT_LO_AT and inside(it - 2):
                    split(it - 2, s)

            def body(it, s):
                for n in range(NB):
                    maxima(it, n, s)
                    behind(it, n, s)

            dve.wait_ge(const_in, 32)
            pairs(dve, body, last_it)
            for it in (ITS, ITS + 1):
                for n in range(NB):
                    behind(it, n, it % 2)


def stage_c(nc, keep, passed, wraw, wo_in, keys, mask, mask_in, x, ident_d, ao_hi, ao_lo, x1, q2_hi, q2_lo):
    k = Kit(nc, "c")
    (const_in, neg_ready, whi_ready, wlo_ready, in0, in1, mm_done, res_ready, chain_s, var_ready, rstd_ready, xn_ready,
     xt_ready, hi_ready, lo_ready, x1_out0, x1_out1, q_out0, q_out1, expo_ready) = semaphores(
        nc, keep, "c", "const_in neg_ready whi_ready wlo_ready in0 in1 mm_done res_ready chain var_ready rstd_ready "
        "xn_ready xt_ready hi_ready lo_ready x1_out0 x1_out1 q_out0 q_out1 expo_ready")
    in_q, x1_out, q_out = [in0, in1], [x1_out0, x1_out1], [q_out0, q_out1]
    NLOAD = 3
    PARTS = 4
    PC = CC // PARTS
    QSCALE = -1.0 / D ** 0.5
    with k.ctx:
        ident = k.sb("ident", [P, P])
        WH = k.sb("WH", [P, 2, CC, 512], F32R)
        WL = k.sb("WL", [P, 2, CC, 512], F32R)
        AH = k.sb("AH", [P, 2, CC, P], F32R)
        AL = k.sb("AL", [P, 2, CC, P], F32R)
        xb = k.sb("x", [P, 2, C])
        res = k.sb("res", [P, 2, C])
        xn = k.sb("xn", [P, C])
        stats = k.sb("stats", [P, 2, 6])
        mv = k.sb("mv", [P, 2])
        veps = k.sb("veps", [P, 1])
        rstd = k.sb("rstd", [P, 1])
        expo = k.sb("expo", [P, 1])
        QH = k.sb("QH", [P, 2, CC, P], F32R)
        QL = k.sb("QL", [P, 2, CC, P], F32R)
        M = k.ps("M", [P, 4, 512])
        T = k.ps("T", [P, 2, CC, P])
        block = k.ctx.enter_context(nc.Block())

        @block.sync
        def _(sp):
            def load(b, qt):
                s = qt % 2
                n = b * QT + qt
                wait(sp, mm_done, 2 * n - 2)
                wait(sp, res_ready, 2 * n - 2)
                for src, dst in ((ao_hi, AH), (ao_lo, AL)):
                    sp.dma_start(dst[:, s, :, :].bitcast(F32),
                                 src[bass.ds(b * C, C), qt * P:(qt + 1) * P]
                                 .rearrange("(c p) t -> p c t", p=P)).then_inc(in_q[s], 16)
                sp.dma_start(xb[:, s, :], x[bass.ds(b * S + qt * P, P), :]).then_inc(in_q[s], 16)

            def store(b, qt):
                s = qt % 2
                n = b * QT + qt
                sp.wait_ge(res_ready, 2 * n + 2)
                sp.dma_start(x1[bass.ds(b * G * S, G * S), :].rearrange("(g q p) c -> q p g c", q=QT, p=P)[qt],
                             res[:, s, :].rearrange("p (g c) -> p g c", g=G)).then_inc(x1_out[s], 16)
                for ready, buf, dst in ((hi_ready, QH, q2_hi), (lo_ready, QL, q2_lo)):
                    sp.wait_ge(ready, n + 1)
                    sp.dma_start(dst[bass.ds(b * C, C), qt * P:(qt + 1) * P].rearrange("(c p) t -> p c t", p=P),
                                 buf[:, s, :, :].bitcast(F32)).then_inc(q_out[s], 16)

            sp.dma_start(ident[:, :], ident_d).then_inc(const_in, 16)
            load(0, 0)
            load(0, 1)
            for qt in range(2):
                load(0, qt + 2)
                store(0, qt)
            with sp.Fori(1, B) as b:
                for qt in range(QT):
                    load(b, qt)
                    store(b - 1, qt + 2) if qt < 2 else store(b, qt - 2)
            store(B - 1, 2)
            store(B - 1, 3)
            for s in range(2):
                sp.wait_ge(x1_out[s], NT // 2 * 16)
                sp.wait_ge(q_out[s], NT // 2 * 32)

        @block.gpsimd
        def _(pool):
            pool.memset(expo[:, :], -0.5).then_inc(expo_ready, 1)
            pool.wait_ge(expo_ready, 1)
            with pool.Fori(0, NT) as t:
                pool.wait_ge(var_ready, t + 1)
                nc.gpsimd.tensor_tensor(out=rstd[:, :], in0=veps[:, :], in1=expo[:, :],
                                        op=ALU.pow).then_inc(rstd_ready, 1)

        @block.scalar
        def _(act):
            act.wait_ge(wo_in, 32)
            for half in range(2):
                for p in range(PARTS):
                    cols = slice(p * PC, (p + 1) * PC)
                    nc.scalar.activation(WH[:, half, cols, :], wraw[:, cols, half * 512:(half + 1) * 512],
                                         ACT.Copy).then_inc(whi_ready, 1)

            def high(b, qt):
                act.wait_ge(xt_ready, b * QT + qt + 1)
                wait(act, q_out[qt % 2], (b * 2 + qt // 2) * 32)
                nc.scalar.activation(QH[:, qt % 2, :, :], T[:, qt % 2, :, :], ACT.Copy,
                                     scale=QSCALE).then_inc(hi_ready, 1)

            for qt in range(QT):
                high(0, qt)
            act.wait_ge(keys.raw_in, 64)
            nc.scalar.activation(keys.K[:, 0, :], keys.raw[:, :], ACT.Copy).then_inc(keys.raw_hi, 1)
            act.wait_ge(mask_in, 16)
            nc.scalar.activation(mask[:, :, :], mask[:, :, :], ACT.Copy, scale=-1.0).then_inc(neg_ready, 1)
            with act.Fori(1, B) as b:
                for qt in range(QT):
                    high(b, qt)

        @block.vector
        def _(dve):
            for half in range(2):
                for p in range(PARTS):
                    cols = slice(p * PC, (p + 1) * PC)
                    dve.wait_ge(whi_ready, half * PARTS + p + 1)
                    nc.vector.tensor_tensor(out=WL[:, half, cols, :], in0=wraw[:, cols, half * 512:(half + 1) * 512],
                                            in1=WH[:, half, cols, :].bitcast(F32),
                                            op=ALU.subtract).then_inc(wlo_ready, 1)
            chain = Chain(dve, chain_s)

            def low(b, qt):
                dve.wait_ge(hi_ready, b * QT + qt + 1)
                nc.vector.scalar_tensor_tensor(out=QL[:, qt % 2, :, :], in0=T[:, qt % 2, :, :], scalar=QSCALE,
                                               in1=QH[:, qt % 2, :, :].bitcast(F32), op0=ALU.mult,
                                               op1=ALU.subtract).then_inc(lo_ready, 1)

            def batch(b):
                chain.base, chain.n = b * 2 * QT, 0
                for qt in range(QT):
                    s = qt % 2
                    n = b * QT + qt
                    dve.wait_ge(in_q[s], (b * 2 + qt // 2 + 1) * 16 * NLOAD)
                    wait(dve, x1_out[s], (b * 2 + qt // 2) * 16)
                    for half in range(2):
                        cols = slice(half * 512, half * 512 + 512)
                        dve.wait_ge(mm_done, 2 * n + half + 1)
                        nc.vector.tensor_tensor(out=res[:, s, cols], in0=M[:, 2 * s + half, :], in1=xb[:, s, cols],
                                                op=ALU.add).then_inc(res_ready, 1)
                    dve.wait_ge(res_ready, 2 * n + 2)
                    nc.vector.bn_stats(stats[:, 0, :], res[:, s, 0:512])
                    chain(nc.vector.bn_stats(stats[:, 1, :], res[:, s, 512:1024]))
                    apart(dve, passed["dve"])
                    chain(nc.vector.bn_aggr(mv[:, :], stats[:, :, :]))
                    nc.vector.tensor_scalar(out=veps[:, :], in0=mv[:, 1:2], scalar1=EPS, scalar2=None,
                                            op0=ALU.add).then_inc(var_ready, 1)
                    dve.wait_ge(rstd_ready, n + 1)
                    wait(dve, xt_ready, n)
                    nc.vector.tensor_scalar(out=xn[:, :], in0=res[:, s, :], scalar1=mv[:, 0:1], scalar2=rstd[:, :],
                                            op0=ALU.subtract, op1=ALU.mult).then_inc(xn_ready, 1)
                    low(b, qt)

            batch(0)
            dve.wait_ge(keys.raw_hi, 1)
            dve.wait_ge(keys.lows_in, 16)
            nc.vector.scalar_tensor_tensor(out=keys.K[:, 0, :], in0=keys.K[:, 0, :].bitcast(F32),
                                           scalar=keys.lows[:, :], in1=keys.raw[:, :], op0=ALU.mult,
                                           op1=ALU.add).then_inc(keys.ready, 1)
            with dve.Fori(1, B) as b:
                batch(b)

        @block.tensor
        def _(pe):
            pe.wait_ge(const_in, 16)

            def rows_t(b, qt):
                pe.wait_ge(xn_ready, b * QT + qt + 1)
                wait(pe, lo_ready, b * QT + qt - 1)
                for c in range(CC):
                    last = nc.tensor.transpose(T[:, qt % 2, c, :], xn[:, c * P:(c + 1) * P], ident[:, :])
                last.then_inc(xt_ready, 1)

            def project(b, qt):
                s = qt % 2
                pe.wait_ge(in_q[s], (b * 2 + qt // 2 + 1) * 16 * NLOAD)
                wait(pe, res_ready, 2 * (b * QT + qt) - 2)
                for half in range(2):
                    for c in range(CC):
                        if isinstance(b, int) and b == 0 and qt == 0 and c % PC == 0:
                            pe.wait_ge(whi_ready, half * PARTS + c // PC + 1)
                            pe.wait_ge(wlo_ready, half * PARTS + c // PC + 1)
                        for q, (a, w) in enumerate(((AH, WH), (AL, WH), (AH, WL))):
                            last = nc.tensor.matmul(M[:, 2 * s + half, :], a[:, s, c, :], w[:, half, c, :],
                                                    start=c == 0 and q == 0, stop=c == CC - 1 and q == 2)
                    last.then_inc(mm_done, 1)

            for qt in range(QT):
                project(0, qt)
                if qt:
                    rows_t(0, qt - 1)
            with pe.Fori(1, B) as b:
                for qt in range(QT):
                    project(b, qt)
                    rows_t(b, qt - 1) if qt else rows_t(b - 1, QT - 1)
            rows_t(B - 1, QT - 1)


def stage_d(nc, keep, passed, keys, mask, ident_d, ctxT, ctxV, q2_hi, q2_lo, x1, x2):
    NB = R * QT
    AHEAD = 3
    NLOAD = 6
    RING = 8
    FULL = (KC - 1) // 4
    USES = []
    for _qt in range(QT):
        for _j in range(R):
            for _g in range(FULL):
                USES.append((("full", _qt, _j, _g), "dve" if _g == 1 else "act"))
        USES.append((("last", _qt), "act"))
        USES.append((("out", _qt), "dve"))
    ORDER = [u for u, _ in USES]
    TOTAL = {e: sum(x == e for _, x in USES) for e in ("act", "dve")}
    FLUSH = ("flush",)
    k = Kit(nc, "d")
    (const_in, in0, in1, sc_done, mx_done, ex_done, tr_done, ev_act, ev_dve,
     pv_done, osb_ready, rinv_ready, part_ready, sum_ready, out0, out1) = semaphores(
        nc, keep, "d", "const_in in0 in1 sc_done mx_done ex_done tr_done ev_act "
        "ev_dve pv_done osb_ready rinv_ready part_ready sum_ready out0 out1")
    in_q, out_q = [in0, in1], [out0, out1]
    kraw, K, lows, kraw_in, kraw_hi, k_ready = keys.raw, keys.K, keys.lows, keys.raw_in, keys.raw_hi, keys.ready
    ev = {"act": ev_act, "dve": ev_dve}

    def count(use, it):
        if use == FLUSH:
            return "dve", ITS * TOTAL["dve"] + 1
        i = ORDER.index(use)
        e = USES[i][1]
        return e, it * TOTAL[e] + sum(x == e for _, x in USES[:i + 1])

    def filled(use, it):
        return it * len(USES) + (1 if use == FLUSH else ORDER.index(use) + 1)

    def slot_of(use):
        return 0 if use == FLUSH else ORDER.index(use) % 3

    def before(use, it):
        i = 0 if use == FLUSH else ORDER.index(use)
        if i >= 3:
            return ORDER[i - 3], it
        return [u for m, u in enumerate(ORDER) if m % 3 == i][-1], it - 1

    with k.ctx:
        ident = k.sb("ident", [P, P])
        Q = k.sb("Q", [P, 2, R, S], F32R)
        V = k.sb("V", [P, 2, KC, D])
        x1b = k.sb("x1", [P, 2, QT, P])
        res = k.sb("res", [P, 2, QT, P])
        prob = k.sb("prob", [P, RING, KP])
        PT = k.sb("PT", [P, 2, KC, R * P])
        nmax = k.sb("nmax", [P, 2, 2, NB])
        rsum = k.sb("rsum", [P, 2, NB])
        rinv = k.sb("rinv", [P, 2, R])
        osb = k.sb("osb", [P, R * P])
        red = k.sb("red", [P, R, D])
        part = k.sb("part", [P, 2, R, D])
        SC = k.ps("SC", [P, 2, 2, 512])
        T = k.ps("T", [P, 3, 512])
        O = k.ps("O", [P, R * P])
        block = k.ctx.enter_context(nc.Block())
        last_it = ITS - 1

        def turn(it, s):
            return it // 2 if isinstance(it, int) else (it - s) // 2

        @block.sync
        def _(sp):
            def load(it, s):
                if not (isinstance(it, int) and it == 0):
                    sp.wait_ge(k_ready, it)
                    for r in range(4):
                        sp.dma_start(kraw[32 * r:32 * r + 32, :], ctxT[bass.ds(it * D, D), :]).then_inc(kraw_in, 16)
                wait(sp, sc_done, (it - 1) * NB * 2)
                apart(sp, passed["sp"])
                wait(sp, pv_done, (it - 1) * QT)
                wait(sp, sum_ready, (it - 1) * QT)
                for r, src in enumerate((q2_hi, q2_hi, q2_lo, q2_lo)):
                    sp.dma_start(Q[32 * r:32 * r + 32, s, :, :].bitcast(F32),
                                 src[bass.ds(it * P, P), :].rearrange("(j p) t -> p j t", p=D)).then_inc(in_q[s], 16)
                sp.dma_start(V[:, s, :, :], ctxV[bass.ds(it * P, P), :, :]).then_inc(in_q[s], 16)
                sp.dma_start(x1b[:, s, :, :], x1[bass.ds(it * S, S), :]
                             .rearrange("(q p) c -> p q c", p=P)).then_inc(in_q[s], 16)

            def store(it, s):
                sp.wait_ge(sum_ready, (it + 1) * QT)
                sp.dma_start(x2[bass.ds(it * S, S), :].rearrange("(q p) c -> p q c", p=P),
                             res[:, s, :, :]).then_inc(out_q[s], 16)

            def body(it, s):
                if not (isinstance(it, int) and it == last_it):
                    load(it + 1, 1 - s)
                if not (isinstance(it, int) and it == 0):
                    store(it - 1, 1 - s)

            sp.dma_start(ident[:, :], ident_d).then_inc(const_in, 16)
            load(0, 0)
            pairs(sp, body, last_it)
            store(last_it, last_it % 2)
            for s in range(2):
                sp.wait_ge(out_q[s], ITS // 2 * 16)

        @block.gpsimd
        def _(pool):
            def add(it, qt, s):
                if qt == 0:
                    wait(pool, out_q[s], turn(it, s) * 16)
                    pool.wait_ge(in_q[s], (turn(it, s) + 1) * 16 * NLOAD)
                pool.wait_ge(part_ready, it * QT + qt + 1)
                nc.gpsimd.tensor_tensor(out=res[:, s, qt, :], in0=part[:, qt % 2, :, :].rearrange("p j d -> p (j d)"),
                                        in1=x1b[:, s, qt, :], op=ALU.add).then_inc(sum_ready, 1)

            def split_keys(it, s):
                pool.wait_ge(kraw_in, (it + 1) * 64)
                wait(pool, sc_done, (it - 1) * NB * 2)
                apart(pool, passed["pool"])
                nc.gpsimd.tensor_copy(K[:, s, :], kraw[:, :]).then_inc(kraw_hi, 1)
                pool.wait_ge(kraw_hi, 2 * it)
                nc.gpsimd.tensor_tensor(out=K[:, s, :], in0=K[:, s, :].bitcast(F32),
                                        in1=lows[:, :].broadcast_to([P, KP]), op=ALU.mult).then_inc(kraw_hi, 1)
                pool.wait_ge(kraw_hi, 2 * it + 1)
                nc.gpsimd.tensor_tensor(out=K[:, s, :], in0=kraw[:, :], in1=K[:, s, :].bitcast(F32),
                                        op=ALU.add).then_inc(k_ready, 1)

            def body(it, s):
                if not (isinstance(it, int) and it == last_it):
                    split_keys(it + 1, 1 - s)
                for qt in range(QT):
                    add(it, qt, s)


            pairs(pool, body, last_it)

        @block.tensor
        def _(pe):
            def scores(it, n, s, half):
                if n == 0 and half == 0:
                    pe.wait_ge(in_q[s], (turn(it, s) + 1) * 16 * NLOAD)
                    pe.wait_ge(k_ready, it + 1)
                qt, j = n // R, n % R
                wait(pe, mx_done, (it * NB + n) * 2 + half - 1)
                for c in range(2):
                    part_ = half * 2 + c
                    last = nc.tensor.matmul(SC[:, half, c, 0:KQ], Q[:, s, j, qt * P:(qt + 1) * P],
                                            K[:, s, part_ * KQ:(part_ + 1) * KQ], start=True, stop=True)
                last.then_inc(sc_done, 1)

            def bank(use, it):
                u, i = before(use, it)
                e, c = count(u, i)
                wait(pe, ev[e], c)
                return slot_of(use)

            def transposes(it, n, g):
                qt, j = n // R, n % R
                if g == 0:
                    pe.wait_ge(ex_done, it * NB + n + 1)
                b = bank(("full", qt, j, g), it)
                for c in range(4):
                    last = nc.tensor.transpose(T[:, b, c * P:(c + 1) * P],
                                               prob[:, n % RING, (4 * g + c) * P:(4 * g + c + 1) * P], ident[:, :])
                last.then_inc(tr_done, 1)

            def last_chunk(it, qt):
                b = bank(("last", qt), it)
                for j in range(R):
                    last = nc.tensor.transpose(T[0:KLAST, b, j * P:(j + 1) * P],
                                               prob[:, (qt * R + j) % RING, (KC - 1) * P:KP], ident[:, :])
                last.then_inc(tr_done, 1)

            def values(it, qt, s, r):
                if r == 0:
                    for use in (("full", qt, R - 1, 2), ("last", qt)):
                        e, c = count(use, it)
                        wait(pe, ev[e], c)
                    wait(pe, osb_ready, it * QT + qt)
                for c in range(4):
                    tile = slice(32 * c, 32 * c + 32)
                    if r < 3:
                        nc.tensor.matmul(O[tile, :], V[:, s, 4 * r + c, :], PT[:, qt % 2, 4 * r + c, :],
                                         start=r == 0, stop=False)
                    else:
                        cols = slice(c * P, (c + 1) * P)
                        last = nc.tensor.matmul(O[tile, cols], V[0:KLAST, s, KC - 1, :],
                                                PT[0:KLAST, qt % 2, KC - 1, cols], start=False, stop=True)
                if r == 3:
                    last.then_inc(pv_done, 1)

            def way_out(it, qt, at, at_it):
                b = bank(at, at_it)
                pe.wait_ge(osb_ready, it * QT + qt + 1)
                for j in range(R):
                    last = nc.tensor.transpose(T[:, b, j * P:(j + 1) * P], osb[:, j * P:(j + 1) * P], ident[:, :])
                last.then_inc(tr_done, 1)

            def body(it, s):
                for n in range(NB):
                    qt, j = n // R, n % R
                    ahead = n + AHEAD
                    for half in range(2):
                        if ahead < NB:
                            scores(it, ahead, s, half)
                        elif not (isinstance(it, int) and it == last_it):
                            scores(it + 1, ahead - NB, 1 - s, half)
                        if half == 0:
                            transposes(it, n, 0)
                            transposes(it, n, 1)
                    transposes(it, n, 2)
                    prev = (it, qt - 1, s) if qt else (it - 1, QT - 1, 1 - s)
                    none = isinstance(it, int) and it == 0 and qt == 0
                    if not none and j < 3:
                        values(*prev, j)
                        if j == 2:
                            values(*prev, 3)
                    if j == R - 1:
                        last_chunk(it, qt)
                        if none:
                            b = bank(("out", 0), 0)
                            for m in range(R):
                                last = nc.tensor.transpose(T[:, b, m * P:(m + 1) * P], prob[:, m, 0:P], ident[:, :])
                            last.then_inc(tr_done, 1)
                        else:
                            way_out(prev[0], prev[1], ("out", qt), it)

            pe.wait_ge(const_in, 16)
            for n in range(AHEAD):
                for half in range(2):
                    scores(0, n, 0, half)
            pairs(pe, body, last_it)
            for r in range(4):
                values(last_it, QT - 1, last_it % 2, r)
            way_out(last_it, QT - 1, FLUSH, ITS)

        @block.scalar
        def _(act):
            def exponent(it, n, s):
                act.wait_ge(mx_done, (it * NB + n + 1) * 2)
                nc.scalar.activation(prob[:, n % RING, :], prob[:, n % RING, :], ACT.Exp,
                                     bias=nmax[:, s, 1, n:n + 1], scale=-1.0,
                                     accum_out=rsum[:, s, n:n + 1]).then_inc(ex_done, 1)

            def evac(it, n, g):
                qt, j = n // R, n % R
                use = ("full", qt, j, g)
                if j == 0 and g == 0:
                    wait(act, pv_done, it * QT + qt - 1)
                act.wait_ge(tr_done, filled(use, it))
                nc.scalar.activation(PT[:, qt % 2, 4 * g:4 * g + 4, j * P:(j + 1) * P],
                                     T[:, slot_of(use), :].rearrange("p (c t) -> p c t", t=P),
                                     ACT.Copy).then_inc(ev_act, 1)

            def evac_last(it, qt):
                act.wait_ge(tr_done, filled(("last", qt), it))
                nc.scalar.activation(PT[0:KLAST, qt % 2, KC - 1, :], T[0:KLAST, slot_of(("last", qt)), :],
                                     ACT.Copy).then_inc(ev_act, 1)

            def copy_out(it, qt):
                act.wait_ge(pv_done, it * QT + qt + 1)
                wait(act, tr_done, filled(("out", qt), it))
                nc.scalar.activation(osb[:, :], O[:, :], ACT.Copy).then_inc(osb_ready, 1)

            def body(it, s):
                last = isinstance(it, int) and it == last_it
                for n in range(NB):
                    qt, j = n // R, n % R
                    if n + 1 < NB:
                        exponent(it, n + 1, s)
                    elif not last:
                        exponent(it + 1, 0, 1 - s)
                    evac(it, n, 0)
                    if j == R - 1 and not (isinstance(it, int) and it == 0 and qt == 0):
                        copy_out(*((it, qt - 1) if qt else (it - 1, QT - 1)))
                    evac(it, n, 2)
                    if j == R - 1:
                        evac_last(it, qt)

            act.wait_ge(const_in, 16)
            exponent(0, 0, 0)
            pairs(act, body, last_it)
            copy_out(last_it, QT - 1)

        @block.vector
        def _(dve):
            def maxima(it, n, s, half):
                qt = n // R
                m = (it * NB + n) * 2 + half
                dve.wait_ge(sc_done, m + 1)
                if half == 0:
                    unit, j = n // R, n % R
                    u = ("last", unit - 2) if unit >= 2 else ("last", unit + 2)
                    i = it if unit >= 2 else it - 1
                    wait(dve, tr_done, filled(u, i))
                    start = 3e38
                else:
                    dve.wait_ge(mx_done, m)
                    start = nmax[:, s, 0, n:n + 1]
                cols = slice(half * 2 * KQ, (half + 1) * 2 * KQ)
                apart(dve, passed["dve"])
                nc.vector.tensor_tensor_reduce(
                    out=prob[:, n % RING, cols].rearrange("p (c k) -> p c k", k=KQ), in0=SC[:, half, :, 0:KQ],
                    in1=mask[:, qt, cols].rearrange("p (c k) -> p c k", k=KQ), scale=1.0, scalar=start,
                    op0=ALU.add, op1=ALU.min, accum_out=nmax[:, s, half, n:n + 1]).then_inc(mx_done, 1)

            def evac(it, use):
                _, qt, j, g = use
                dve.wait_ge(tr_done, filled(use, it))
                if j == 0:
                    wait(dve, pv_done, it * QT + qt - 1)
                nc.vector.tensor_copy(PT[:, qt % 2, 4 * g:4 * g + 4, j * P:(j + 1) * P],
                                      T[:, slot_of(use), :].rearrange("p (c t) -> p c t", t=P)).then_inc(ev_dve, 1)

            def finish(it, qt, s, use, at_it):
                dve.wait_ge(tr_done, filled(use, at_it))
                n = it * QT + qt
                wait(dve, part_ready, n)
                nc.vector.tensor_reduce(out=red[:, :, :], in_=T[:, slot_of(use), :]
                                        .rearrange("p (j k d) -> p j d k", j=R, k=4), axis=AX.X,
                                        op=ALU.add).then_inc(ev_dve, 1)
                nc.vector.reciprocal(rinv[:, qt % 2, :], rsum[:, s, qt * R:(qt + 1) * R]).then_inc(rinv_ready, 1)
                dve.wait_ge(ev_dve, count(use, at_it)[1])
                dve.wait_ge(rinv_ready, n + 1)
                wait(dve, sum_ready, n - 1)
                nc.vector.tensor_tensor(out=part[:, qt % 2, :, :], in0=red[:, :, :],
                                        in1=rinv[:, qt % 2, :].unsqueeze(2).broadcast_to([P, R, D]),
                                        op=ALU.mult).then_inc(part_ready, 1)

            def body(it, s):
                last = isinstance(it, int) and it == last_it
                for n in range(NB):
                    qt, j = n // R, n % R
                    ahead = n + AHEAD
                    for half in range(2):
                        if ahead < NB:
                            maxima(it, ahead, s, half)
                        elif not last:
                            maxima(it + 1, ahead - NB, 1 - s, half)
                        if half == 0:
                            evac(it, ("full", qt, j, 1))
                    if j == R - 1:
                        if isinstance(it, int) and it == 0 and qt == 0:
                            dve.wait_ge(tr_done, filled(("out", 0), 0))
                            nc.vector.tensor_copy(osb0[:, :], T[:, slot_of(("out", 0)), 0:1]).then_inc(ev_dve, 1)
                        elif qt:
                            finish(it, qt - 1, s, ("out", qt), it)
                        else:
                            finish(it - 1, QT - 1, 1 - s, ("out", 0), it)

            osb0 = red[:, 0, 0:1]
            dve.wait_ge(const_in, 16)
            for n in range(AHEAD):
                for half in range(2):
                    maxima(0, n, 0, half)
            pairs(dve, body, last_it)
            finish(last_it, QT - 1, last_it % 2, FLUSH, ITS)


def stage_e(nc, keep, passed, ident_d, w1_d, wrT_d, keysT_d, avT_d, wvdT_d, wvuT_d, low_half, vecs_d, scal_d, x2, out):
    N1 = BOT + HU
    outer = Kit(nc, "e")
    (const_in, wuh_ready, wul_ready, pad_ready, ident_in, w1_in, in0, in1, in2, in3, chain_s, var_ready,
     rstd_ready, hn_ready, xt_ready, ht_ready, um_ready, sum_ready,
     q_ready, qt_done, qt_ready, cube_ready, tanh_ready, learn_ready, expo_ready, rk_done, rk_ready, av_done,
     av_ready) = semaphores(
        nc, keep, "e", "const_in wuh_ready wul_ready pad_ready ident_in w1_in in0 in1 in2 in3 chain var_ready "
        "rstd_ready hn_ready xt_ready ht_ready um_ready "
        "sum_ready q_ready qt_done qt_ready cube_ready tanh_ready learn_ready expo_ready rk_done rk_ready av_done "
        "av_ready")
    in_q = [in0, in1, in2, in3]
    NORM, CUBE, LEARN = 3, 3, 2
    NCONST = 9
    last_t = NT - 1
    with outer.ctx:
        ident = outer.sb("ident", [P, P])
        X2 = outer.sb("X2", [P, NT, C])
        keysT = outer.sb("keysT", [BOT, NS])
        wrT = outer.sb("wrT", [BOT, RD])
        rkT = outer.sb("rkT", [RD, NS])
        AV = outer.sb("AV", [P, 2, 2 * BOT])
        lows = outer.sb("lows", [2 * BOT, 1])
        WUH = outer.sb("WUH", [2 * BOT, C], F32R)
        WUL = outer.sb("WUL", [2 * BOT, C], F32R)
        vecs = outer.sb("vecs", [P, 3, NS])
        scal = outer.sb("scal", [P, 3])
        QT_ = outer.sb("QT", [BOT, TOK + P])
        varh = outer.sb("varh", [P, NT])
        learn = outer.sb("learn", [P, NT])
        log_rel, bu1, wu2 = vecs[:, 0, :], vecs[:, 1, :], vecs[:, 2, :]

        k = Kit(nc, "e1")
        with k.ctx:
            w1 = k.sb("w1", [P, CC, N1])
            avT = k.sb("avT", [P, CC, NS])
            wvdT = k.sb("wvdT", [P, CC, BOT])
            wvuT = k.sb("wvuT", [2 * BOT, C])
            stats = k.sb("stats", [P, 2, 6])
            mv = k.sb("mv", [P, 2])
            veps = k.sb("veps", [P, 1])
            rstd = k.sb("rstd", [P, 1])
            expo = k.sb("expo", [P, 1])
            hn = k.sb("hn", [P, 2, C])
            hT = k.sb("hT", [P, 2, CC, P])
            qsb = k.sb("qsb", [P, 2, BOT])
            y = k.sb("y", [P, 2, HU])
            y2 = k.sb("y2", [P, HU])
            y3 = k.sb("y3", [P, 2, HU])
            th = k.sb("th", [P, 2, HU])
            half_y = k.sb("half_y", [P, 2, HU])
            lrn = k.sb("lrn", [P, 1])
            T = k.ps("T", [P, 2, CC, P])
            U = k.ps("U", [P, 2, 512])
            QP = k.ps("QP", [P, 512])
            AP_ = k.ps("AVP", [P, 512])
            block = k.ctx.enter_context(nc.Block())

            @block.sync
            def _(sp):
                def load(b):
                    for qt in range(QT):
                        wait(sp, in_q[qt], b * 16)
                        sp.dma_start(X2[:, bass.ds(b * QT + qt, 1), :].rearrange("p o (g c) -> p (o g) c", g=G),
                                     x2[bass.ds(b * G * S, G * S), :]
                                     .rearrange("(g q p) c -> q p g c", q=QT, p=P)[qt]).then_inc(in_q[qt], 16)

                sp.dma_start(ident[:, :], ident_d).then_inc(ident_in, 16)
                load(0)
                sp.dma_start(w1[:, :, :], w1_d).then_inc(w1_in, 16)
                for dst, src in ((wrT, wrT_d), (keysT, keysT_d), (avT, avT_d), (wvdT, wvdT_d),
                                 (wvuT[0:BOT], wvuT_d), (wvuT[BOT:2 * BOT], wvuT_d), (lows, low_half)):
                    sp.dma_start(dst[:], src).then_inc(const_in, 16)
                sp.dma_start(vecs[:, :, :].rearrange("p a b -> p (a b)"), vecs_d.partition_broadcast(P)).then_inc(const_in, 16)
                sp.dma_start(scal[:, :], scal_d.partition_broadcast(P)).then_inc(const_in, 16)
                with sp.Fori(1, B) as b:
                    load(b)

            @block.gpsimd
            def _(pool):
                pool.memset(expo[:, :], -0.5).then_inc(expo_ready, 1)
                pool.wait_ge(expo_ready, 1)

                def body(t, m):
                    pool.wait_ge(var_ready, t + 1)
                    nc.gpsimd.tensor_tensor(out=rstd[:, :], in0=veps[:, :], in1=expo[:, :],
                                            op=ALU.pow).then_inc(rstd_ready, 1)
                    pool.wait_ge(hn_ready, t + 1)
                    x_t = X2[:, bass.ds(t, 1), :].rearrange("p o c -> p (o c)")
                    nc.gpsimd.tensor_tensor(out=x_t, in0=hn[:, m % 2, :], in1=x_t, op=ALU.add).then_inc(sum_ready, 1)
                fours(pool, body, 4)

            @block.tensor
            def _(pe):
                pe.wait_ge(ident_in, 16)

                def tables():
                    pe.wait_ge(const_in, NCONST * 16)
                    nc.tensor.matmul(AP_[0:RD, 2 * BOT:2 * BOT + NS], wrT[:, :], keysT[:, :], start=True,
                                     stop=True).then_inc(rk_done, 1)
                    for m in range(2):
                        for c in range(CC):
                            last = nc.tensor.matmul(AP_[:, m * BOT:(m + 1) * BOT], avT[:, c, m * P:(m + 1) * P],
                                                    wvdT[:, c, :], start=c == 0, stop=c == CC - 1)
                    last.then_inc(av_done, 1)

                def rows_t(t, m):
                    pe.wait_ge(hn_ready, t + 1)
                    wait(pe, ht_ready, t - 1)
                    for c in range(CC):
                        last = nc.tensor.transpose(T[:, m % 2, c, :], hn[:, m % 2, c * P:(c + 1) * P], ident[:, :])
                    last.then_inc(xt_ready, 1)

                def project(t, m):
                    pe.wait_ge(ht_ready, t + 1)
                    wait(pe, q_ready, t - 1)
                    wait(pe, cube_ready, t - 1)
                    if isinstance(t, int) and t == 0:
                        pe.wait_ge(w1_in, 16)
                    for c in range(CC):
                        last = nc.tensor.matmul(U[:, m % 2, 0:N1], hT[:, m % 2, c, :], w1[:, c, :], start=c == 0,
                                                stop=c == CC - 1)
                    last.then_inc(um_ready, 1)

                def query_t(t, m):
                    pe.wait_ge(q_ready, t + 1)
                    wait(pe, qt_ready, t)
                    apart(pe, passed["pe"])
                    nc.tensor.transpose(QP[0:BOT, 0:P], qsb[:, m % 2, :], ident[:, :]).then_inc(qt_done, 1)

                def body(t, m):
                    if inside(t):
                        rows_t(t, m)
                    if inside(t - 1):
                        project(t - 1, m + 1)
                    if inside(t - 2):
                        query_t(t - 2, m)
                    if isinstance(t, int) and t == QT - 1:
                        tables()
                fours(pe, body, 4, 2)

            @block.scalar
            def _(act):
                def tables():
                    act.wait_ge(rk_done, 1)
                    act.wait_ge(av_done, 1)
                    nc.scalar.activation(rkT[:, :], AP_[0:RD, 2 * BOT:2 * BOT + NS], ACT.Copy).then_inc(rk_ready, 1)
                    for twice in range(2):
                        nc.scalar.activation(AV[:, :, twice * BOT:(twice + 1) * BOT],
                                             AP_[:, 0:2 * BOT].rearrange("p (a b) -> p a b", a=2),
                                             ACT.Copy).then_inc(av_ready, 1)
                    act.wait_ge(const_in, NCONST * 16)
                    nc.scalar.activation(WUH[:, :], wvuT[:, :], ACT.Copy).then_inc(wuh_ready, 1)

                def copy_t(t, m):
                    act.wait_ge(xt_ready, t + 1)
                    wait(act, um_ready, t - 1)
                    nc.scalar.activation(hT[:, m % 2, :, :], T[:, m % 2, :, :], ACT.Copy).then_inc(ht_ready, 1)

                def query(t, m):
                    act.wait_ge(um_ready, t + 1)
                    wait(act, qt_done, t - 1)
                    nc.scalar.activation(qsb[:, m % 2, :], U[:, m % 2, 0:BOT], ACT.Copy).then_inc(q_ready, 1)

                def tanh(t, m):
                    act.wait_ge(cube_ready, t + 1)
                    wait(act, learn_ready, t - 1)
                    nc.scalar.activation(th[:, m % 2, :], y3[:, m % 2, :], ACT.Tanh,
                                         scale=0.7978845608028654).then_inc(tanh_ready, 1)

                def query_out(t):
                    act.wait_ge(qt_done, t + 1)
                    nc.scalar.activation(QT_[:, bass.ds(t * P, P)], QP[0:BOT, 0:P], ACT.Copy).then_inc(qt_ready, 1)

                def body(t, m):
                    if inside(t):
                        copy_t(t, m)
                    if inside(t - 2):
                        tanh(t - 2, m)
                    if inside(t - 1):
                        query(t - 1, m + 1)
                    if inside(t - 2):
                        query_out(t - 2)
                    if isinstance(t, int) and t == QT - 1:
                        tables()
                fours(act, body, 4, 2)

            @block.vector
            def _(dve):
                chain = Chain(dve, chain_s)
                nc.vector.memset(QT_[:, TOK:], 0.0).then_inc(pad_ready, 1)
                dve.wait_ge(pad_ready, 1)

                def tile_of(t):
                    return X2[:, bass.ds(t, 1), :].rearrange("p o c -> p (o c)")

                def moments(t, m):
                    dve.wait_ge(in_q[m], ((t // QT if isinstance(t, int) else (t - m) // QT) + 1) * 16)
                    nc.vector.bn_stats(stats[:, 0, :], tile_of(t)[:, 0:512])
                    chain(nc.vector.bn_stats(stats[:, 1, :], tile_of(t)[:, 512:1024]))
                    apart(dve, passed["dve"])
                    chain(nc.vector.bn_aggr(mv[:, :], stats[:, :, :]))
                    nc.vector.tensor_scalar(out=veps[:, :], in0=mv[:, 1:2], scalar1=EPS, scalar2=None,
                                            op0=ALU.add).then_inc(var_ready, 1)

                def norm(t, m):
                    dve.wait_ge(rstd_ready, t + 1)
                    chain(nc.vector.tensor_scalar(out=varh[:, bass.ds(t, 1)], in0=mv[:, 1:2], scalar1=rstd[:, :],
                                                  scalar2=rstd[:, :], op0=ALU.mult, op1=ALU.mult))
                    wait(dve, xt_ready, t - 1)
                    wait(dve, sum_ready, t - 1)
                    nc.vector.tensor_scalar(out=hn[:, m % 2, :], in0=tile_of(t), scalar1=mv[:, 0:1],
                                            scalar2=rstd[:, :], op0=ALU.subtract,
                                            op1=ALU.mult).then_inc(hn_ready, 1)

                def cube(t, m):
                    dve.wait_ge(q_ready, t + 1)
                    chain(nc.vector.tensor_tensor(out=y[:, m % 2, :], in0=U[:, m % 2, BOT:N1], in1=bu1, op=ALU.add))
                    chain(nc.vector.tensor_tensor(out=y2[:, :], in0=y[:, m % 2, :], in1=y[:, m % 2, :], op=ALU.mult))
                    chain(nc.vector.tensor_scalar(out=y2[:, :], in0=y2[:, :], scalar1=0.044715, scalar2=1.0,
                                                  op0=ALU.mult, op1=ALU.add))
                    wait(dve, tanh_ready, t - 1)
                    nc.vector.tensor_tensor(out=y3[:, m % 2, :], in0=y2[:, :], in1=y[:, m % 2, :],
                                            op=ALU.mult).then_inc(cube_ready, 1)

                def learned(t, m):
                    dve.wait_ge(tanh_ready, t + 1)
                    chain(nc.vector.scalar_tensor_tensor(out=half_y[:, 0, :], in0=th[:, m % 2, :], scalar=1.0,
                                                         in1=y[:, m % 2, :], op0=ALU.add, op1=ALU.mult))
                    apart(dve, passed["dve"])
                    chain(nc.vector.tensor_tensor_reduce(out=half_y[:, 1, :], in0=half_y[:, 0, :], in1=wu2, scale=0.5,
                                                         scalar=0.0, op0=ALU.mult, op1=ALU.add, accum_out=lrn[:, :]))
                    nc.vector.tensor_copy(learn[:, bass.ds(t, 1)], lrn[:, :]).then_inc(learn_ready, 1)

                def body(t, m):
                    if isinstance(t, int):
                        chain.base = (NORM * min(t, NT) + CUBE * min(max(t - 2, 0), NT)
                                      + LEARN * min(max(t - 3, 0), NT))
                    else:
                        chain.base = t * (NORM + CUBE + LEARN) - (2 * CUBE + 3 * LEARN)
                    chain.n = 0
                    if inside(t):
                        moments(t, m)
                    if inside(t - 3):
                        learned(t - 3, m + 1)
                    if inside(t):
                        norm(t, m)
                    if isinstance(t, int) and t == 2:
                        dve.wait_ge(const_in, NCONST * 16)
                    if isinstance(t, int) and t == NT:
                        dve.wait_ge(wuh_ready, 1)
                        nc.vector.tensor_tensor(out=WUL[:, :], in0=wvuT[:, :], in1=WUH[:, :].bitcast(F32),
                                                op=ALU.subtract).then_inc(wul_ready, 1)
                    if inside(t - 2):
                        cube(t - 2, m)
                fours(dve, body, 4, 3)

        stage_e2(nc, keep, passed, ident, X2, keysT, wrT, rkT, AV, lows, WUH, WUL, log_rel, scal, QT_, varh, learn, out)


def inside(t):
    return not isinstance(t, int) or 0 <= t < NT


def fours(eng, body, lead, behind=0):
    for t in range(lead):
        body(t, t % 4)
    with eng.Fori(lead // 4, NT // 4) as b:
        for m in range(4):
            body(b * 4 + m, m)
    for t in range(NT, NT + behind):
        body(t, t % 4)


def stage_e2(nc, keep, passed, ident, X2, keysT, wrT, rkT, AV, lows, WUH, WUL, log_rel, scal, QT_, varh, learn, out):
    (ones_ready, log_ready, tot_done, chain_s, sig_in, sig_out, gate_in, gate_out, gate_ready, q_ready, rq_done,
     rq_ready, ra_done, pick_ready, chain1_s, chain2_s, w_ready, wt_done, wt_ready, tv_done, tvh_ready,
     tv_ready, o_done, o_ready, out0, out1) = semaphores(
        nc, keep, "f", "ones_ready log_ready tot_done chain sig_in sig_out gate_in gate_out gate_ready q_ready "
        "rq_done rq_ready ra_done pick_ready chain1 chain2 w_ready wt_done wt_ready tv_done tvh_ready "
        "tv_ready o_done o_ready out0 out1")
    out_q = [out0, out1]
    PICK, FIN = 7, 2
    GATES_AT = 3
    LEAD, BEHIND = 8, 4
    k = Kit(nc, "f")
    with k.ctx:
        ones = k.sb("ones", [P, P])
        logv = k.sb("logv", [P, NT])
        lsum = k.sb("lsum", [P, 1])
        mean = k.sb("mean", [P, 1])
        half_l = k.sb("half_l", [P, NT])
        sig = k.sb("sig", [P, NT])
        u = k.sb("u", [P, NT])
        gate = k.sb("gate", [P, NT])
        big = k.sb("big", [P, NT])
        q_s = k.sb("q_s", [BOT, 2, P])
        rq = k.sb("rq", [RD, P])
        rs = k.sb("rs", [P, NS])
        top = k.sb("top", [P, 8])
        rep = k.sb("rep", [P, NS])
        at = k.sb("at", [P, NS])
        att = k.sb("att", [P, 2, NS])
        amax = k.sb("amax", [P, 1])
        nmax = k.sb("nmax", [P, 2])
        w = k.sb("w", [P, 2, NS])
        wsum = k.sb("wsum", [P, 4])
        wt = k.sb("wt", [P, 2, P])
        tvh = k.sb("tvh", [2 * BOT, P], F32R)
        tv = k.sb("tv", [2 * BOT, P], F32R)
        rws = k.sb("rws", [P, 1])
        fac = k.sb("fac", [P, 1])
        ob = k.sb("ob", [P, 2, C])
        TOT = k.ps("TOT", [P, 512])
        RQ = k.ps("RQ", [P, 512])
        RA = k.ps("RA", [P, 2, NS])
        WT = k.ps("WT", [P, 512])
        TV = k.ps("TV", [P, 512])
        OUT = k.ps("OUT", [P, 2, 512])
        block = k.ctx.enter_context(nc.Block())

        @block.sync
        def _(sp):
            def body(t, m):
                sp.wait_ge(o_ready, 2 * t + 2)
                sp.dma_start(out[bass.ds(t * P, P), :], ob[:, m % 2, :]).then_inc(out_q[m % 2], 16)
            fours(sp, body, 4)
            for s in range(2):
                sp.wait_ge(out_q[s], NT // 2 * 16)

        @block.tensor
        def _(pe):
            pe.wait_ge(ones_ready, 1)
            pe.wait_ge(log_ready, 1)
            nc.tensor.matmul(TOT[:, 0:1], ones[:, :], lsum[:, :], start=True, stop=True).then_inc(tot_done, 1)

            def route(t, m):
                pe.wait_ge(q_ready, t + 1)
                wait(pe, rq_ready, t)
                apart(pe, passed["pe"])
                nc.tensor.matmul(RQ[0:RD, 0:P], wrT[:, :], q_s[:, m % 2, :], start=True, stop=True).then_inc(rq_done, 1)

            def scores(t, m):
                pe.wait_ge(rq_ready, t + 1)
                if not (isinstance(t, int) and t == 0):
                    pe.wait_ge(chain1_s, (t - 1) * PICK + 2)
                nc.tensor.matmul(RA[:, 0, :], rq[:, :], rkT[:, :], start=True, stop=True)
                nc.tensor.matmul(RA[:, 1, :], q_s[:, m % 2, :], keysT[:, :], start=True, stop=True).then_inc(ra_done, 1)

            def up(t):
                pe.wait_ge(tv_ready, t + 1)
                for half in range(2):
                    wait(pe, o_ready, 2 * t + half - 1)
                    cols = slice(half * 512, (half + 1) * 512)
                    nc.tensor.matmul(OUT[:, half, :], tv[:, :], WUH[:, cols], start=True, stop=False)
                    nc.tensor.matmul(OUT[:, half, :], tv[:, :], WUL[:, cols], start=False, stop=True).then_inc(o_done, 1)

            def weights_t(t, m):
                pe.wait_ge(w_ready, t + 1)
                wait(pe, wt_ready, t)
                for c in range(2):
                    last = nc.tensor.transpose(WT[:, c * P:(c + 1) * P], w[:, m % 2, c * P:(c + 1) * P], ident[:, :])
                last.then_inc(wt_done, 1)

            def down(t):
                pe.wait_ge(wt_ready, t + 1)
                wait(pe, tv_ready, t)
                for c in range(2):
                    last = nc.tensor.matmul(TV[:, 0:P], AV[:, c, :], wt[:, c, :], start=c == 0, stop=c == 1)
                last.then_inc(tv_done, 1)

            def body(t, m):
                if inside(t):
                    route(t, m)
                if inside(t - 1):
                    scores(t - 1, m + 1)
                if inside(t - 4):
                    up(t - 4)
                if inside(t - 3):
                    down(t - 3)
                if inside(t - 2):
                    weights_t(t - 2, m)
            fours(pe, body, LEAD, BEHIND)

        @block.scalar
        def _(act):
            nc.scalar.activation(logv[:, :], varh[:, :], ACT.Ln, bias=1.0, accum_out=lsum[:, :]).then_inc(log_ready, 1)
            act.wait_ge(sig_in, 1)
            nc.scalar.activation(sig[:, :], half_l[:, :], ACT.Tanh).then_inc(sig_out, 1)

            def query(t, m):
                wait(act, ra_done, t - 1)
                nc.scalar.activation(q_s[:, m % 2, :], QT_[:, bass.ds(t * P, P)], ACT.Copy).then_inc(q_ready, 1)

            def routed(t):
                act.wait_ge(rq_done, t + 1)
                wait(act, ra_done, t)
                nc.scalar.activation(rq[:, :], RQ[0:RD, 0:P], ACT.Copy).then_inc(rq_ready, 1)

            def weights(t, m):
                act.wait_ge(pick_ready, t + 1)
                wait(act, wt_done, t - 1)
                wait(act, o_ready, 2 * (t - 3))
                nc.scalar.activation(w[:, m % 2, :], att[:, m % 2, :], ACT.Exp, bias=nmax[:, m % 2:m % 2 + 1],
                                     accum_out=wsum[:, m:m + 1]).then_inc(w_ready, 1)

            def lowered(t):
                act.wait_ge(tv_done, t + 1)
                wait(act, tv_ready, t)
                nc.scalar.activation(tvh[:, :], TV[:, 0:P], ACT.Copy).then_inc(tvh_ready, 1)

            def turned(t):
                act.wait_ge(wt_done, t + 1)
                wait(act, tv_done, t)
                nc.scalar.activation(wt[:, :, :].rearrange("p a b -> p (a b)"), WT[:, 0:2 * P],
                                     ACT.Copy).then_inc(wt_ready, 1)

            def body(t, m):
                if inside(t):
                    routed(t)
                if inside(t + 1):
                    query(t + 1, m + 1)
                if inside(t - 3):
                    lowered(t - 3)
                if inside(t - 1):
                    weights(t - 1, (m - 1) % 4)
                if inside(t - 2):
                    turned(t - 2)
                if isinstance(t, int) and t == GATES_AT:
                    act.wait_ge(gate_in, 1)
                    nc.scalar.activation(gate[:, :], u[:, :], ACT.Tanh).then_inc(gate_out, 1)
            query(0, 0)
            fours(act, body, LEAD, BEHIND)

        @block.vector
        def _(dve):
            chain = Chain(dve, chain_s)
            nc.vector.memset(ones[:, :], 1.0).then_inc(ones_ready, 1)
            nc.vector.tensor_scalar(out=half_l[:, :], in0=learn[:, :], scalar1=scal[:, 0:1], scalar2=0.5,
                                    op0=ALU.add, op1=ALU.mult).then_inc(sig_in, 1)

            def gates():
                dve.wait_ge(tot_done, 1)
                chain(nc.vector.tensor_scalar(out=mean[:, :], in0=TOT[:, 0:1], scalar1=1.0 / TOK, scalar2=1e-6,
                                              op0=ALU.mult, op1=ALU.add))
                chain(nc.vector.reciprocal(mean[:, :], mean[:, :]))
                chain(nc.vector.tensor_scalar(out=u[:, :], in0=logv[:, :], scalar1=mean[:, :], scalar2=0.5,
                                              op0=ALU.mult, op1=ALU.mult))
                dve.wait_ge(sig_out, 1)
                chain(nc.vector.tensor_scalar(out=sig[:, :], in0=sig[:, :], scalar1=1.25, scalar2=1.25,
                                              op0=ALU.mult, op1=ALU.add))
                chain(nc.vector.tensor_tensor(out=u[:, :], in0=u[:, :], in1=sig[:, :], op=ALU.add))
                chain(nc.vector.tensor_scalar(out=u[:, :], in0=u[:, :], scalar1=0.0, scalar2=5.0,
                                              op0=ALU.max, op1=ALU.min))
                chain(nc.vector.tensor_scalar(out=u[:, :], in0=u[:, :], scalar1=0.5, scalar2=1.0 / 1.5,
                                              op0=ALU.subtract, op1=ALU.mult))
                chain(nc.vector.tensor_scalar(out=u[:, :], in0=u[:, :], scalar1=0.0, scalar2=1.0,
                                              op0=ALU.max, op1=ALU.min))
                chain(nc.vector.tensor_scalar(out=u[:, :], in0=u[:, :], scalar1=scal[:, 1:2], scalar2=scal[:, 2:3],
                                              op0=ALU.mult, op1=ALU.add))
                nc.vector.tensor_scalar(out=u[:, :], in0=u[:, :], scalar1=0.5, scalar2=None,
                                        op0=ALU.mult).then_inc(gate_in, 1)
                dve.wait_ge(gate_out, 1)
                chain(nc.vector.tensor_scalar(out=gate[:, :], in0=gate[:, :], scalar1=0.5, scalar2=0.5,
                                              op0=ALU.mult, op1=ALU.add))
                chain(nc.vector.tensor_scalar(out=big[:, :], in0=gate[:, :], scalar1=0.05, scalar2=None, op0=ALU.is_ge))
                nc.vector.tensor_tensor(out=gate[:, :], in0=gate[:, :], in1=big[:, :], op=ALU.mult).then_inc(gate_ready, 1)
                dve.wait_ge(gate_ready, 1)

            chain1, chain2 = Chain(dve, chain1_s), Chain(dve, chain2_s)

            def step(t, m):
                a, ma, f, mf = t - 1, (m - 1) % 4, t - 4, m
                pick, finish = inside(a), inside(f)
                chain1.base, chain1.n = a * PICK, 0
                chain2.base, chain2.n = f * FIN, 0

                def out_half(half):
                    dve.wait_ge(o_done, 2 * f + half + 1)
                    nc.vector.scalar_tensor_tensor(
                        out=ob[:, mf % 2, half * 512:(half + 1) * 512], in0=OUT[:, half, :], scalar=fac[:, :],
                        in1=X2[:, bass.ds(f, 1), half * 512:(half + 1) * 512].rearrange("p o c -> p (o c)"),
                        op0=ALU.mult, op1=ALU.add).then_inc(o_ready, 1)

                if pick:
                    dve.wait_ge(ra_done, a + 1)
                    chain1.mark(nc.vector.scalar_tensor_tensor(out=rs[:, :], in0=RA[:, 0, :], scalar=RD ** -0.5,
                                                                 in1=log_rel, op0=ALU.mult, op1=ALU.add))
                    chain1.mark(nc.vector.scalar_tensor_tensor(out=at[:, :], in0=RA[:, 1, :], scalar=BOT ** -0.5,
                                                                 in1=log_rel, op0=ALU.mult, op1=ALU.add))
                if finish:
                    dve.wait_ge(w_ready, f + 1)
                    wait(dve, o_ready, 2 * f)
                    chain2.mark(nc.vector.reciprocal(rws[:, :], wsum[:, mf:mf + 1]))
                if pick:
                    chain1.settle()
                    apart(dve, passed["dve"])
                    chain1.mark(nc.vector.max(top[:, :], rs[:, :]))
                if finish:
                    chain2.settle()
                    chain2.mark(nc.vector.tensor_tensor(out=fac[:, :], in0=rws[:, :], in1=gate[:, bass.ds(f, 1)],
                                                          op=ALU.mult))
                if pick:
                    chain1.settle()
                    apart(dve, passed["dve"])
                    chain1.mark(nc.vector.match_replace(rep[:, :], top[:, :], rs[:, :], -3e38))
                if finish:
                    chain2.settle()
                    wait(dve, out_q[mf % 2], (f // 2 if isinstance(f, int) else (f - mf % 2) // 2) * 16)
                    out_half(0)
                if pick:
                    chain1.settle()
                    chain1(nc.vector.tensor_tensor(out=rep[:, :], in0=rep[:, :], in1=rs[:, :], op=ALU.not_equal))
                    chain1.mark(nc.vector.tensor_scalar(out=rep[:, :], in0=rep[:, :], scalar1=1.0, scalar2=BIG,
                                                          op0=ALU.subtract, op1=ALU.mult))
                if finish:
                    out_half(1)
                if pick:
                    chain1.settle()
                    wait(dve, w_ready, a - 1)
                    apart(dve, passed["dve"])
                    chain1.mark(nc.vector.tensor_tensor_reduce(out=att[:, ma % 2, :], in0=at[:, :], in1=rep[:, :],
                                                                 scale=1.0, scalar=-3e38, op0=ALU.add, op1=ALU.max,
                                                                 accum_out=amax[:, :]))
                    chain1.settle()
                    nc.vector.tensor_scalar(out=nmax[:, ma % 2:ma % 2 + 1], in0=amax[:, :], scalar1=-1.0,
                                            scalar2=None, op0=ALU.mult).then_inc(pick_ready, 1)
                    dve.wait_ge(pick_ready, a + 1)

            def low(t):
                dve.wait_ge(tvh_ready, t + 1)
                wait(dve, o_done, 2 * t)
                nc.vector.scalar_tensor_tensor(out=tv[:, :], in0=tvh[:, :].bitcast(F32), scalar=lows[:, :],
                                               in1=TV[:, 0:P], op0=ALU.mult, op1=ALU.add).then_inc(tv_ready, 1)

            def body(t, m):
                step(t, m)
                if inside(t - 3):
                    low(t - 3)
                if isinstance(t, int) and t == GATES_AT:
                    gates()
            fours(dve, body, LEAD, BEHIND)


def program(nc, a, out):
    qk_hi = nc.dram_tensor("qk_hi", [2 * B * C, S], F32, kind="Internal").ap()
    qk_lo = nc.dram_tensor("qk_lo", [2 * B * C, S], F32, kind="Internal").ap()
    v_dram = nc.dram_tensor("v_dram", [ITS * S, P], F32, kind="Internal").ap()
    ao_hi = nc.dram_tensor("ao_hi", [B * C, S], F32, kind="Internal").ap()
    ao_lo = nc.dram_tensor("ao_lo", [B * C, S], F32, kind="Internal").ap()
    x1 = nc.dram_tensor("x1", [ITS * S, P], F32, kind="Internal").ap()
    x2 = nc.dram_tensor("x2", [ITS * S, P], F32, kind="Internal").ap()
    q2_hi = nc.dram_tensor("q2_hi", [B * C, S], F32, kind="Internal").ap()
    q2_lo = nc.dram_tensor("q2_lo", [B * C, S], F32, kind="Internal").ap()
    with ExitStack() as keep:
        passed = dict(zip(("pe", "dve", "pool", "sp"), semaphores(nc, keep, "passed", "pe dve pool sp")))
        stage_a(nc, keep, passed, a["x"], a["wqkvT"], a["rope"], a["ident"], qk_hi, qk_lo, v_dram)
        cross, proj = Kit(nc, "cross"), Kit(nc, "proj")
        mask_in, wo_in = semaphores(nc, keep, "early", "mask_in wo_in")
        with cross.ctx:
            mask = cross.sb("mask", [P, QT, KP])
            keys = Keys(nc, keep, cross)
            with proj.ctx:
                wo = proj.sb("wo", [P, CC, C])
                wo_d, half = a["woT"].rearrange("(c p) n -> p c n", p=P), CC // 2
                early = {0: ((wo[:, :half, :], wo_d[:, :half, :], wo_in),),
                         1: ((wo[:, half:, :], wo_d[:, half:, :], wo_in),),
                         ITS - 1: (*((keys.raw[r * D:(r + 1) * D, :], a["ctxT"][0:D, :], keys.raw_in)
                                     for r in range(4)),
                                   (keys.lows[:, :], a["low_rows"], keys.lows_in),
                                   (mask[:, :, :], a["mask"], mask_in))}
                stage_b(nc, keep, passed, early, a["ident"], a["causal"], qk_hi, qk_lo, v_dram, ao_hi, ao_lo)
                stage_c(nc, keep, passed, wo, wo_in, keys, mask, mask_in, a["x"], a["ident"], ao_hi, ao_lo, x1,
                        q2_hi, q2_lo)
            stage_d(nc, keep, passed, keys, mask, a["ident"], a["ctxT"], a["ctxV"], q2_hi, q2_lo, x1, x2)
        stage_e(nc, keep, passed, a["ident"], a["w1"], a["wrT"], a["keysT"], a["avT"], a["wvdT"], a["wvuT"], a["low_half"], a["vecs"],
                a["scal"], x2, out)


def constants():
    import numpy as np
    f = np.float32
    theta = (f(1.0) / f(10000.0) ** (np.arange(0, D, 2, dtype=f) / f(D))).astype(f)
    angle = np.outer(np.arange(S, dtype=f), theta).astype(f)
    angle = np.concatenate([angle, angle], -1)
    cos, sin = np.cos(angle).astype(f), np.sin(angle).astype(f)
    sin[:, :D // 2] *= -1
    scale = f(-1.0 / np.sqrt(D))
    tab = np.stack([np.stack([cos * scale, sin * scale]), np.stack([cos, sin])]).astype(f)
    rope = np.ascontiguousarray(tab.reshape(2, 2, QT, P, D).transpose(3, 0, 1, 2, 4))
    causal = np.zeros((P, S), f)
    causal[:, S - P:] = np.where(np.arange(P)[None, :] > np.arange(P)[:, None], f(BIG), f(0))
    return {"ident": np.eye(P, dtype=f), "rope": rope, "causal": causal,
            "low_half": np.repeat(np.array([0, -1], f), BOT).reshape(2 * BOT, 1),
            "low_rows": np.repeat(np.array([0, -1, 0, -1], f), D).reshape(P, 1)}


def layout(i):
    import numpy as np
    g = {n: np.asarray(v) for n, v in i.items()}

    def chunks(w):
        return np.ascontiguousarray(w.reshape(CC, P, -1).transpose(1, 0, 2))

    ctx = g["ctx_1024"]
    keys = np.zeros((B, KC * P, G, D), ctx.dtype)
    keys[:, :KEYS] = ctx.reshape(B, KEYS, G, D)
    mask = np.full((S, KP), -BIG, np.float32)
    mask[:, :KEYS] = g["mask_SxS2_ff0"]
    return {
        "x": g["x"].reshape(TOK, C),
        "woT": np.ascontiguousarray(g["L0_attn_wo"].T),
        "ctxT": np.ascontiguousarray(keys[:, :KP].transpose(0, 2, 3, 1)).reshape(ITS * D, KP),
        "ctxV": np.ascontiguousarray(keys.reshape(B, KC, P, G, D).transpose(0, 3, 2, 1, 4)).reshape(ITS * P, KC, D),
        "mask": np.ascontiguousarray(mask.reshape(QT, P, KP).transpose(1, 0, 2)),
        "wqkvT": np.ascontiguousarray(np.concatenate([g["L0_attn_wq"], g["L0_attn_wk"], g["L0_attn_wv"]]).T),
        "w1": chunks(np.concatenate([g["L0_ffn_Wq"], g["L0_ffn_Wu1"]]).T),
        "wrT": np.ascontiguousarray(g["L0_ffn_Wr"].T),
        "keysT": np.ascontiguousarray(g["L0_ffn_aux_keys"].T),
        "avT": chunks(g["L0_ffn_aux_values"].T),
        "wvdT": chunks(g["L0_ffn_Wvd"].T),
        "wvuT": np.ascontiguousarray(g["L0_ffn_Wvu"].T),
        "vecs": np.concatenate([g["L0_ffn_log_rel"], g["L0_ffn_bu1"], g["L0_ffn_Wu2"][0]]),
        "scal": np.concatenate([g["L0_ffn_bu2"], g["L0_ffn_gate_w1"].reshape(1), g["L0_ffn_gate_bias"].reshape(1)]),
        **constants(),
    }


def kernel(**inputs):
    import numpy as np
    import concourse.bacc as bacc
    from concourse.bass_utils import run_bass_kernel_spmd

    nc = bacc.Bacc("TRN2", target_bir_lowering=False, num_devices=1)
    arrays = layout(inputs)
    aps = {n: nc.dram_tensor(f"in_{n}", v.shape, mybir.dt.from_np(v.dtype), kind="ExternalInput").ap()
           for n, v in arrays.items()}
    out = nc.dram_tensor("out_x", [TOK, C], F32, kind="ExternalOutput").ap()
    program(nc, aps, out)
    r = run_bass_kernel_spmd(nc, [{f"in_{n}": v for n, v in arrays.items()}], core_ids=[0])
    return np.asarray(r.results[0]["out_x"]).reshape(B, S, C)
```
